# Optimizing a Trainium2 kernel written in Bass

```python
import numpy as np
import jax
import jax.numpy as jnp

def _softmax(x, axis=-1):
    return jax.nn.softmax(x, axis=axis)

def _gelu(x):
    return jax.nn.gelu(x, approximate=True)

def _silu(x):
    return jax.nn.silu(x)

def _sigmoid(x):
    return jax.nn.sigmoid(x)

def _layernorm(x, axis=-1, eps=1e-05):
    m = jnp.mean(x, axis=axis, keepdims=True)
    v = jnp.var(x, axis=axis, keepdims=True)
    return (x - m) / jnp.sqrt(v + eps)

def _scatter_add(tgt, idx, src, axis=0):
    return tgt.at[idx].add(src)

def _segment_sum(src, seg, n):
    return jax.ops.segment_sum(src, seg, n)
kernel_name = 'mk_metaformer_d2_conv_nhwc768_r4_fcccb0'

def setup_inputs(seed: int=0):
    np.random.seed(seed)
    _w = jnp.asarray

    def _rec_inputs():
        import jax
        import jax.numpy as jnp
        _gk = jax.random.key(seed)
        x = -0.0002221 + 1 * jax.random.normal(jax.random.fold_in(_gk, 1), (8, 16, 16, 192), jnp.float32)
        return x
    x = _rec_inputs()

    def _L0_conv_setup():
        import jax, jax.numpy as jnp
        import numpy as np
        WS = 14
        NH = 12
        DIM = 192
        key = jax.random.key(seed)
        ks = jax.random.split(key, 6)
        hd = DIM // NH
        return {'x': jax.random.normal(ks[0], (8, 16, 16, DIM), jnp.float32), 'qkv_w': jax.random.normal(ks[1], (3 * DIM, DIM), jnp.float32) * 0.02, 'qkv_b': jnp.zeros((3 * DIM,), jnp.float32), 'proj_w': jax.random.normal(ks[2], (DIM, DIM), jnp.float32) * 0.02, 'proj_b': jnp.zeros((DIM,), jnp.float32), 'rel_pos_h': jax.random.normal(ks[3], (2 * WS - 1, hd), jnp.float32) * 0.02, 'rel_pos_w': jax.random.normal(ks[4], (2 * WS - 1, hd), jnp.float32) * 0.02}
    _L0_conv_all = _L0_conv_setup()
    _L0_conv_in = {k: v for k, v in _L0_conv_all.items() if k in ('qkv_w', 'qkv_b', 'proj_w', 'proj_b', 'rel_pos_h', 'rel_pos_w')}
    del _L0_conv_all

    def _L0_ffn_setup():
        import jax, jax.numpy as jnp
        import numpy as np
        B, T, D = (4, 512, 192)
        E, F, K = (8, 4 * 192, 2)
        key = jax.random.key(seed)
        ks = jax.random.split(key, 5)
        s = 0.02
        return {'x': jax.random.normal(ks[0], (B, T, D), dtype=jnp.float32), 'Wg': jax.random.normal(ks[1], (D, E), dtype=jnp.float32) * s, 'bg': jnp.zeros((E,), dtype=jnp.float32), 'W1': jax.random.normal(ks[2], (E, D, F), dtype=jnp.float32) * s, 'b1': jnp.zeros((E, F), dtype=jnp.float32), 'W2': jax.random.normal(ks[3], (E, F, D), dtype=jnp.float32) * s, 'b2': jnp.zeros((E, D), dtype=jnp.float32)}
    _L0_ffn_all = _L0_ffn_setup()
    _L0_ffn_in = {k: v for k, v in _L0_ffn_all.items() if k in ('Wg', 'bg', 'W1', 'b1', 'W2', 'b2')}
    del _L0_ffn_all

    def _L1_conv_setup():
        import jax, jax.numpy as jnp
        import numpy as np
        KSZ = 3
        DILATIONS = (1, 2, 3)
        G = 4

        def _unfold(x, k, dil):
            B, C, H, W = x.shape
            pad = dil * (k - 1) // 2
            xp = jnp.pad(x, ((0, 0), (0, 0), (pad, pad), (pad, pad)))
            patches = jnp.stack([xp[:, :, i * dil:i * dil + H, j * dil:j * dil + W] for i in range(k) for j in range(k)], axis=2)
            return patches

        def _dilate_attention(q, k, v, head_dim, scale, ksz, dil):
            B, d, H, W = q.shape
            nh = d // head_dim
            L = H * W
            kk = ksz * ksz
            qr = q.reshape(B, nh, head_dim, L)
            kp = _unfold(k, ksz, dil).reshape(B, nh, head_dim, kk, L)
            vp = _unfold(v, ksz, dil).reshape(B, nh, head_dim, kk, L)
            attn = jnp.einsum('bncl,bnckl->bnlk', qr, kp) * scale
            attn = jax.nn.softmax(attn, axis=-1)
            out = jnp.einsum('bnlk,bnckl->bnlc', attn, vp)
            return jnp.transpose(out, (0, 2, 1, 3)).reshape(B, H, W, d)

        def _forward(x, qkv_w, proj_w, proj_b):
            B, H, W, C = x.shape
            nd = len(DILATIONS)
            gd = C // G
            hd = gd // nd
            scale = hd ** (-0.5)
            xc = jnp.transpose(x, (0, 3, 1, 2))
            xg = xc.reshape(G, B, gd, H, W)
            outs = []
            for g in range(G):
                qkv = jnp.einsum('oi,bihw->bohw', qkv_w, xg[g])
                qkv = qkv.reshape(nd, 3, B, gd // 3, H, W)
                for i in range(nd):
                    outs.append(_dilate_attention(qkv[i, 0], qkv[i, 1], qkv[i, 2], hd, scale, KSZ, DILATIONS[i]))
            y = jnp.stack(outs).reshape(B, H, W, C)
            return y @ proj_w.T + proj_b
        key = jax.random.key(seed)
        k1, k2, k3 = jax.random.split(key, 3)
        B, H, W, C = (4, 16, 16, 192)
        gd = C // G
        x = jax.random.normal(k1, (B, H, W, C), dtype=jnp.float32)
        qkv_w = jax.random.normal(k2, (3 * gd, gd), dtype=jnp.float32) * 0.02
        proj_w = jax.random.normal(k3, (C, C), dtype=jnp.float32) * 0.02
        proj_b = jnp.zeros((C,), dtype=jnp.float32)
        return {'x': x, 'qkv_w': qkv_w, 'proj_w': proj_w, 'proj_b': proj_b}
    _L1_conv_all = _L1_conv_setup()
    _L1_conv_in = {k: v for k, v in _L1_conv_all.items() if k in ('qkv_w', 'proj_w', 'proj_b')}
    del _L1_conv_all

    def _L1_ffn_setup():
        import jax, jax.numpy as jnp
        import numpy as np
        TOP_K = 2
        key = jax.random.key(seed)
        ks = jax.random.split(key, 5)
        B, S, D, H, E = (1, 512, 192, 768, 8)
        x = jax.random.normal(ks[0], (B, S, D), dtype=jnp.float32)
        gate_w = jax.random.normal(ks[1], (E, D), dtype=jnp.float32) * 0.02
        w1 = jax.random.normal(ks[2], (E, D, H), dtype=jnp.float32) * 0.02
        b1 = jnp.zeros((E, H), dtype=jnp.float32)
        w2 = jax.random.normal(ks[3], (E, H, D), dtype=jnp.float32) * 0.02
        b2 = jnp.zeros((E, D), dtype=jnp.float32)
        return {'x': x, 'gate_w': gate_w, 'w1': w1, 'b1': b1, 'w2': w2, 'b2': b2}
    _L1_ffn_all = _L1_ffn_setup()
    _L1_ffn_in = {k: v for k, v in _L1_ffn_all.items() if k in ('gate_w', 'w1', 'b1', 'w2', 'b2')}
    del _L1_ffn_all
    return {'x': x, 'L0_conv_qkv_w': _L0_conv_in['qkv_w'], 'L0_conv_qkv_b': _L0_conv_in['qkv_b'], 'L0_conv_proj_w': _L0_conv_in['proj_w'], 'L0_conv_proj_b': _L0_conv_in['proj_b'], 'L0_conv_rel_pos_h': _L0_conv_in['rel_pos_h'], 'L0_conv_rel_pos_w': _L0_conv_in['rel_pos_w'], 'L0_ffn_Wg': _L0_ffn_in['Wg'], 'L0_ffn_bg': _L0_ffn_in['bg'], 'L0_ffn_W1': _L0_ffn_in['W1'], 'L0_ffn_b1': _L0_ffn_in['b1'], 'L0_ffn_W2': _L0_ffn_in['W2'], 'L0_ffn_b2': _L0_ffn_in['b2'], 'L1_conv_qkv_w': _L1_conv_in['qkv_w'], 'L1_conv_proj_w': _L1_conv_in['proj_w'], 'L1_conv_proj_b': _L1_conv_in['proj_b'], 'L1_ffn_gate_w': _L1_ffn_in['gate_w'], 'L1_ffn_w1': _L1_ffn_in['w1'], 'L1_ffn_b1': _L1_ffn_in['b1'], 'L1_ffn_w2': _L1_ffn_in['w2'], 'L1_ffn_b2': _L1_ffn_in['b2']}

def reference(x, L0_conv_qkv_w, L0_conv_qkv_b, L0_conv_proj_w, L0_conv_proj_b, L0_conv_rel_pos_h, L0_conv_rel_pos_w, L0_ffn_Wg, L0_ffn_bg, L0_ffn_W1, L0_ffn_b1, L0_ffn_W2, L0_ffn_b2, L1_conv_qkv_w, L1_conv_proj_w, L1_conv_proj_b, L1_ffn_gate_w, L1_ffn_w1, L1_ffn_b1, L1_ffn_w2, L1_ffn_b2):
    import jax
    import jax.numpy as jnp

    def _L0_conv_ref(x, qkv_w, qkv_b, proj_w, proj_b, rel_pos_h, rel_pos_w):
        import jax, jax.numpy as jnp
        import numpy as np
        WS = 14
        NH = 12
        DIM = 192
        B, H, W, C = x.shape
        ws, nh = (WS, NH)
        hd = C // nh
        scale = hd ** (-0.5)
        pad_h = -H % ws
        pad_w = -W % ws
        xp = jnp.pad(x, ((0, 0), (0, pad_h), (0, pad_w), (0, 0)))
        Hp, Wp = (H + pad_h, W + pad_w)
        nwh, nww = (Hp // ws, Wp // ws)
        win = xp.reshape(B, nwh, ws, nww, ws, C).transpose(0, 1, 3, 2, 4, 5)
        win = win.reshape(B * nwh * nww, ws, ws, C)
        Bw = win.shape[0]
        N = ws * ws
        qkv = win.reshape(Bw, N, C) @ qkv_w.T + qkv_b
        qkv = qkv.reshape(Bw, N, 3, nh, hd).transpose(2, 0, 3, 1, 4)
        qkv = qkv.reshape(3, Bw * nh, N, hd)
        q, k, v = (qkv[0], qkv[1], qkv[2])
        attn = jnp.einsum('bnd,bmd->bnm', q * scale, k)
        coords = jnp.arange(ws)[:, None] - jnp.arange(ws)[None, :] + (ws - 1)
        Rh = rel_pos_h[coords]
        Rw = rel_pos_w[coords]
        rq = q.reshape(Bw * nh, ws, ws, hd)
        rel_h = jnp.einsum('bhwc,hkc->bhwk', rq, Rh)
        rel_w = jnp.einsum('bhwc,wkc->bhwk', rq, Rw)
        attn = (attn.reshape(-1, ws, ws, ws, ws) + rel_h[:, :, :, :, None] + rel_w[:, :, :, None, :]).reshape(-1, N, N)
        attn = jax.nn.softmax(attn, axis=-1)
        out = (attn @ v).reshape(Bw, nh, ws, ws, hd).transpose(0, 2, 3, 1, 4)
        out = out.reshape(Bw, ws, ws, C)
        out = out @ proj_w.T + proj_b
        xo = out.reshape(B, nwh, nww, ws, ws, C).transpose(0, 1, 3, 2, 4, 5)
        xo = xo.reshape(B, Hp, Wp, C)
        return xo[:, :H, :W, :]

    def _L0_ffn_ref(x, Wg, bg, W1, b1, W2, b2):
        import jax, jax.numpy as jnp
        import numpy as np
        B, T, D = (4, 512, 192)
        E, F, K = (8, 4 * 192, 2)
        b, t, d = x.shape
        x_flat = x.reshape(-1, d)
        n = x_flat.shape[0]
        gates = jax.nn.softmax(x_flat @ Wg + bg, axis=-1)
        topk_g, topk_i = jax.lax.top_k(gates, K)
        combine = jnp.zeros((n, W1.shape[0]), dtype=gates.dtype)
        combine = combine.at[jnp.arange(n)[:, None], topk_i].add(topk_g)
        h = jnp.einsum('nd,edf->enf', x_flat, W1) + b1[:, None, :]
        h = jax.nn.gelu(h, approximate=False)
        y = jnp.einsum('enf,efd->end', h, W2) + b2[:, None, :]
        out = jnp.einsum('ne,end->nd', combine, y)
        return out.reshape(b, t, d)

    def _L1_conv_ref(x, qkv_w, proj_w, proj_b):
        import jax, jax.numpy as jnp
        import numpy as np
        KSZ = 3
        DILATIONS = (1, 2, 3)
        G = 4

        def _unfold(x, k, dil):
            B, C, H, W = x.shape
            pad = dil * (k - 1) // 2
            xp = jnp.pad(x, ((0, 0), (0, 0), (pad, pad), (pad, pad)))
            patches = jnp.stack([xp[:, :, i * dil:i * dil + H, j * dil:j * dil + W] for i in range(k) for j in range(k)], axis=2)
            return patches

        def _dilate_attention(q, k, v, head_dim, scale, ksz, dil):
            B, d, H, W = q.shape
            nh = d // head_dim
            L = H * W
            kk = ksz * ksz
            qr = q.reshape(B, nh, head_dim, L)
            kp = _unfold(k, ksz, dil).reshape(B, nh, head_dim, kk, L)
            vp = _unfold(v, ksz, dil).reshape(B, nh, head_dim, kk, L)
            attn = jnp.einsum('bncl,bnckl->bnlk', qr, kp) * scale
            attn = jax.nn.softmax(attn, axis=-1)
            out = jnp.einsum('bnlk,bnckl->bnlc', attn, vp)
            return jnp.transpose(out, (0, 2, 1, 3)).reshape(B, H, W, d)

        def _forward(x, qkv_w, proj_w, proj_b):
            B, H, W, C = x.shape
            nd = len(DILATIONS)
            gd = C // G
            hd = gd // nd
            scale = hd ** (-0.5)
            xc = jnp.transpose(x, (0, 3, 1, 2))
            xg = xc.reshape(G, B, gd, H, W)
            outs = []
            for g in range(G):
                qkv = jnp.einsum('oi,bihw->bohw', qkv_w, xg[g])
                qkv = qkv.reshape(nd, 3, B, gd // 3, H, W)
                for i in range(nd):
                    outs.append(_dilate_attention(qkv[i, 0], qkv[i, 1], qkv[i, 2], hd, scale, KSZ, DILATIONS[i]))
            y = jnp.stack(outs).reshape(B, H, W, C)
            return y @ proj_w.T + proj_b
        return _forward(x, qkv_w, proj_w, proj_b)

    def _L1_ffn_ref(x, gate_w, w1, b1, w2, b2):
        import jax, jax.numpy as jnp
        import numpy as np
        TOP_K = 2
        B, S, D = x.shape
        E, _, H = w1.shape
        T = B * S
        K = TOP_K
        xf = x.reshape(T, D)
        logits = xf @ gate_w.T
        probs = jax.nn.softmax(logits, axis=-1)
        top_w, top_i = jax.lax.top_k(probs, K)
        top_w = top_w / (jnp.sum(top_w, axis=-1, keepdims=True) + 1e-09)
        flat_e = top_i.reshape(-1)
        flat_w = top_w.reshape(-1)
        tok_idx = jnp.repeat(jnp.arange(T), K)
        order = jnp.argsort(flat_e)
        se = flat_e[order]
        pt = tok_idx[order]
        pw = flat_w[order]
        counts = jax.ops.segment_sum(jnp.ones(T * K, jnp.int32), se, num_segments=E)
        starts = jnp.concatenate([jnp.zeros((1,), jnp.int32), jnp.cumsum(counts)[:-1]])
        pos = jnp.arange(T * K) - starts[se]
        cap = T * K
        padded = jnp.zeros((E, cap, D), x.dtype).at[se, pos].set(xf[pt])
        hidden = jax.nn.gelu(jnp.einsum('ecd,edh->ech', padded, w1) + b1[:, None, :], approximate=False)
        out = jnp.einsum('ech,ehd->ecd', hidden, w2) + b2[:, None, :]
        expert_out = out[se, pos] * pw[:, None]
        final = jnp.zeros((T, D), x.dtype).at[pt].add(expert_out)
        return final.reshape(B, S, D)

    def _gn(v, G=32, eps=1e-05):
        B_, H_, W_, C_ = v.shape
        g = v.reshape(B_, H_, W_, G, C_ // G)
        m = jnp.mean(g, axis=(1, 2, 4), keepdims=True)
        s = jnp.var(g, axis=(1, 2, 4), keepdims=True)
        return ((g - m) / jnp.sqrt(s + eps)).reshape(v.shape)

    def _ln_c(v, eps=1e-06):
        m = jnp.mean(v, axis=-1, keepdims=True)
        s = jnp.var(v, axis=-1, keepdims=True)
        return (v - m) / jnp.sqrt(s + eps)

    def _ln_t(v, eps=1e-05):
        m = jnp.mean(v, axis=-1, keepdims=True)
        s = jnp.var(v, axis=-1, keepdims=True)
        return (v - m) / jnp.sqrt(s + eps)

    def _to_tokens(v):
        B_, H_, W_, C_ = v.shape
        return v.reshape(B_, H_ * W_, C_)

    def _from_tokens(t, like):
        return t.reshape(like.shape)
    x = x + _L0_conv_ref(_ln_c(x), L0_conv_qkv_w, L0_conv_qkv_b, L0_conv_proj_w, L0_conv_proj_b, L0_conv_rel_pos_h, L0_conv_rel_pos_w)
    t = _to_tokens(x)
    t = t + _L0_ffn_ref(_ln_t(t), L0_ffn_Wg, L0_ffn_bg, L0_ffn_W1, L0_ffn_b1, L0_ffn_W2, L0_ffn_b2)
    x = _from_tokens(t, x)
    x = x + _L1_conv_ref(_ln_c(x), L1_conv_qkv_w, L1_conv_proj_w, L1_conv_proj_b)
    t = _to_tokens(x)
    t = t + _L1_ffn_ref(_ln_t(t), L1_ffn_gate_w, L1_ffn_w1, L1_ffn_b1, L1_ffn_w2, L1_ffn_b2)
    x = _from_tokens(t, x)
    return x

_drawn_inputs = setup_inputs


def setup_inputs(seed=0):
    import zlib

    import numpy as np

    out = dict(_drawn_inputs(seed))
    spreads = {'L0_conv_qkv_b': (0.0, 0.1),
     'L0_conv_proj_b': (0.0, 0.1),
     'L0_ffn_bg': (0.0, 0.451),
     'L0_ffn_b1': (0.0, 0.718),
     'L0_ffn_b2': (0.0, 0.297),
     'L1_conv_proj_b': (0.0, 0.1),
     'L1_ffn_b1': (0.0, 0.374),
     'L1_ffn_b2': (0.0, 0.1)}
    factors = {'L0_conv_qkv_w': 7.129,
     'L0_conv_rel_pos_h': 8.0,
     'L0_conv_rel_pos_w': 8.0,
     'L1_conv_qkv_w': 3.927,
     'L1_conv_proj_w': 3.82}
    for name, (base, spread) in spreads.items():
        noise = np.random.default_rng([zlib.crc32(name.encode()), seed]).standard_normal(out[name].shape)
        drawn = base * np.exp(spread * noise) if base else spread * noise
        out[name] = jnp.asarray(drawn.astype(out[name].dtype))
    for name, factor in factors.items():
        out[name] = (out[name] * factor).astype(out[name].dtype)
    return out
```

```python
from contextlib import ExitStack

import concourse.bass as bass
from concourse import mybir

F32 = mybir.dt.float32
F32R = mybir.dt.float32r
BF16 = mybir.dt.bfloat16
I32 = mybir.dt.int32
ALU = mybir.AluOpType
ACT = mybir.ActivationFunctionType
AX = mybir.AxisListType

P = 128
IMGS, SIDE, C = 8, 16, 192
PIX = SIDE * SIDE
T = IMGS * PIX
TILES = T // P
KC = 96
BLKS = 4
BT = T // BLKS
TPB = BT // P
NEG = -float(2 ** 30)

WS, NH, HD = 14, 12, 16
WA = WS * WS
WAH = WA // 2
NBD = SIDE * (SIDE - WS)
NBC = (SIDE - WS) * WS
NB1 = NBD + NBC
NB = 2 * NB1
PADS = 240
HG = 6
HC = 3
CPB = NH // HC
CHUNKS = BLKS * CPB
QROWS = HD + 2 * WS
VW = HG * HD + HG
VS = HG * (HD + VW)
R_HI, R_REL1, R_DUP, R_REL2, R_LO, R_RELLO = 0, 16, 32, 48, 64, 80
R_ROUND = 108
R_WIN = 108
K_MAX = 114
R_MAX = 114

DIL = (1, 2, 3)
GRP, GCH = 4, C // 4
SPU = 8
SUB = 4
L1_ROWS = 96
VW1 = SUB * HD + SUB
VS1 = SUB * (HD + VW1)

E, F, FT = 8, 768, 768 // P
SLOTS = 42
MT = (2 * T - E) // P + E
W1C, W2C = 2 * F, FT * C
LN_EPS = (1e-6, 1e-5, 1e-6, 1e-5)




def build(nc, a, out):
    ctx = ExitStack()
    with ctx:
        def sb(name, shape, dt=F32):
            return ctx.enter_context(nc.sbuf_tensor(name, shape, dt))

        def sem(name):
            return ctx.enter_context(nc.semaphore(name))

        def dram(name, shape):
            return nc.dram_tensor(name, shape, F32, kind="Internal").ap()

        qd = dram("qd", [NH, QROWS, T])
        kd = dram("kd", [NH, HD, T])
        kpd = dram("kpd", [NH, HD, PADS])
        xnd = [dram(f"xnd{l}", [T, C]) for l in range(2)]
        yd = [dram(f"yd{l}", [2 * T, C]) for l in range(2)]
        qkvd = dram("qkvd", [SPU * 3 * len(DIL), GRP, HD, PIX])
        y1d = dram("y1d", [GRP * len(DIL) * SPU, PIX, HD])

        x_sb = sb("x_sb", [P, TILES, C])
        xnT = sb("xnT", [P, 4096])
        xnT_v = xnT[0:KC, :].rearrange("p (k t) -> p k t", k=2)
        xn = sb("xn", [P, 2, TPB, C])
        cst = sb("cst", [P, a["cst"].shape[1]])
        wv0 = sb("wv0", [KC, 2, C])
        wp = [sb(f"wp{l}", [KC, 2, C]) for l in range(2)]
        bp = [sb(f"bp{l}", [P, C]) for l in range(2)]
        bv0 = sb("bv0", [P, C])
        wqkv1 = sb("wqkv1", [KC, 3, KC])
        wg = [sb(f"wg{l}", [KC, 2, E]) for l in range(2)]
        bg = [sb(f"bg{l}", [P, E]) for l in range(2)]
        bqk0 = sb("bqk0", [KC, 4])
        stats = sb("stats", [P, 2, TPB, 6])
        mv = sb("mv", [P, 2, TPB, 2])
        rstd = sb("rstd", [P, 2, TPB])
        veps = sb("veps", [P, 2, TPB])
        newton = sb("newton", [P, 2, TPB])
        credit = sb("credit", [1, 16])
        arena = sb("arena", [P, E * (W1C + W2C)])
        qq = sb("qq", [P, 6144], F32R)
        kk = sb("kk", [P, 6144], F32R)
        pk = sb("pk", [P, NH, PADS], F32R)
        nm = sb("nm", [SPU, 2, BT], F32R)
        gw = sb("gw", [P, 2, TILES])
        gidx = sb("gidx", [P, SLOTS], I32)
        sidx = sb("sidx", [P, SLOTS], I32)
        gcur = sb("gcur", [P, 3], I32)
        scur = sb("scur", [P, 3], I32)
        te = sb("te", [1, SLOTS], I32)
        rt = sb("rt", [P, 2816])
        cstb = sb("cstb", [P, 3 * P + 2 * 32 + SLOTS], BF16)
        smallb = sb("smallb", [P, 64], BF16)
        hotb = sb("hotb", [P, 2 * TILES * E], BF16)
        hotb_v = hotb[:, :].rearrange("p (c e) -> p c e", e=E)
        ROUTE_STEPS = [0]
        ps = ctx.enter_context(nc.psum_tensor("ps", [P, 8, 512], F32))

        at = 0
        CST, CST_AT = {}, {}
        for name, n in (("ident", 128), ("tri", 128), ("iot", 128), ("ones", 128), ("rev", E), ("lt", E * E),
                        ("j128", 16), ("ida", 32), ("idb", 32), ("iots", SLOTS), ("npad", 6), ("pf", 6), ("sel", KC)):
            CST[name], CST_AT[name] = cst[:, at:at + n], at
            at += n
        ident = CST["ident"]
        trib, iotb, onesb = (cstb[:, i * P:(i + 1) * P] for i in range(3))
        idab, idbb, iotsb = cstb[:, 384:416], cstb[:, 416:448], cstb[:, 448:448 + SLOTS]

        def ar(word, shape, parts=P):
            n = 1
            for s in shape:
                n *= s
            v = arena[0:parts, word:word + n]
            names = "abcd"[:len(shape)]
            if len(shape) > 1:
                v = v.rearrange(f"p ({' '.join(names)}) -> p {' '.join(names)}",
                                **{k: s for k, s in zip(names, shape)})
            return v

        def xt_(word, shape, parts=P):
            n = 1
            for s in shape:
                n *= s
            v = xnT[0:parts, word:word + n]
            names = "abcd"[:len(shape)]
            if len(shape) > 1:
                v = v.rearrange(f"p ({' '.join(names)}) -> p {' '.join(names)}",
                                **{k: s for k, s in zip(names, shape)})
            return v

        padf = ar(0, [NH, PADS])
        qT = ar(2880, [2, T], KC)
        pt = [ar(6976 + 2048 * i, [T]) for i in range(3)]
        rn = [ar(13120 + 2048 * i, [T]) for i in range(2)]
        cq = ar(13120, [BT])
        ck = ar(13120 + 512, [BT])
        kpz = ar(13120 + 1024, [PADS], KC)
        kps = ar(13120 + 1024 + PADS, [2, PADS], KC)
        relt = [ar(17216 + 1176 * i, [WS, HG * WS], KC) for i in range(2)]
        wqk0 = ar(19568, [2, 4, KC], KC)
        fq = [ar(1536 * i, [HC, BT]) for i in range(2)]
        fk = [ar(3072 + 1536 * i, [HC, BT]) for i in range(2)]
        v0 = ar(6144, [2, 5, VS])
        pa = [ar(13224 + 1144 * i, [2, 2 * WA]) for i in range(2)]
        pb = [ar(13224 + 1144 * i + 784, [3, NB]) for i in range(2)]
        osb = ar(15512, [BT])
        ot = ar(16536, [2, BT], KC)
        vpad = ar(17560, [2, VS])
        xp = ar(18976, [2, BT], KC)
        mxa = ar(20000, [2, 4, HC])
        mxb = ar(20024, [2, HC])

        w1s = ar(0, [E, 2, F], KC + 1)
        w2s = ar(E * W1C, [E, FT, C])
        wcur = [[xt_(F * r, [F], KC + 1), rt[0:KC + 1, F * r:F * (r + 1)]] for r in range(3)]
        hidT = xt_(3 * F, [FT, P])
        xgT = xt_(4 * F, [2, P], KC + 1)
        xg = [xt_(4 * F + 2 * P + C * r, [C]) for r in range(3)]
        ys = [xt_(4 * F + 2 * P + C * 3, [C])] + [rt[:, 3 * F + C * r:3 * F + C * (r + 1)] for r in range(2)]
        b2s = xn[:, :, :, :].rearrange("p u t c -> p (u t) c")
        yt = ar(0, [TILES, 2, C])

        q0 = qq[:, :].rearrange("p (c h n) -> p c h n", c=CPB, h=HC)
        k0 = kk[:, :].rearrange("p (c h n) -> p c h n", c=CPB, h=HC)

        S = {}

        def s_(name):
            if name not in S:
                S[name] = sem(name)
            return S[name]

        def blocks_of(v):
            return v.rearrange("p (b i y x) -> p b i y x", b=BLKS, i=2, y=SIDE)

        block = ctx.enter_context(nc.Block())

        def ln_vector(v, n):
            for turn in range(2):
                for u in range(2):
                    for j in range(TPB):
                        t = (turn * 2 + u) * TPB + j
                        last = nc.vector.bn_stats(stats[:, u, j, :], x_sb[:, t, :])
                last.then_inc(s_("ln_stats"), 1)
                v.wait_ge(s_("ln_stats"), n * 2 + turn + 1)
                for u in range(2):
                    for j in range(TPB):
                        last = nc.vector.bn_aggr(mv[:, u, j, :], stats[:, u, j, :])
                last.then_inc(s_("ln_mv"), 1)
                v.wait_ge(s_("ln_mv"), n * 2 + turn + 1)
                nc.vector.tensor_scalar(veps[:], mv[:, :, :, 1], LN_EPS[n], None, ALU.add).then_inc(s_("ln_eps"), 1)
                v.wait_ge(s_("ln_sqrt"), n * 2 + turn + 1)
                nc.vector.reciprocal(rstd[:], rstd[:]).then_inc(s_("ln_step"), 1)
                done = (n * 2 + turn) * 4
                v.wait_ge(s_("ln_step"), done + 1)
                nc.vector.tensor_tensor(newton[:], rstd[:], rstd[:], ALU.mult).then_inc(s_("ln_step"), 1)
                v.wait_ge(s_("ln_step"), done + 2)
                nc.vector.tensor_tensor(newton[:], newton[:], veps[:], ALU.mult).then_inc(s_("ln_step"), 1)
                v.wait_ge(s_("ln_step"), done + 3)
                nc.vector.tensor_scalar(newton[:], newton[:], -0.5, 1.5, ALU.mult, ALU.add).then_inc(s_("ln_step"), 1)
                v.wait_ge(s_("ln_step"), done + 4)
                nc.vector.tensor_tensor(rstd[:], rstd[:], newton[:], ALU.mult).then_inc(s_("ln_rstd"), 1)
                v.wait_ge(s_("ln_rstd"), n * 2 + turn + 1)
                for u in range(2):
                    b = turn * 2 + u
                    v.wait_ge(s_("xn_free"), n * BLKS + b + 1)
                    kept = {1: turn, 2: 2, 3: 2 + turn}.get(n, 0)
                    if kept:
                        v.wait_ge(s_(f"xn_kept{u}"), kept * 16)
                    for j in range(TPB):
                        last = nc.vector.tensor_scalar(xn[:, u, j, :], x_sb[:, b * TPB + j, :], mv[:, u, j, 0:1],
                                                       rstd[:, u, j:j + 1], ALU.subtract, ALU.mult)
                    last.then_inc(s_("xn_ready"), 1)

        def ln_transpose(pe, n, b, u):
            pe.wait_ge(s_("xn_ready"), n * BLKS + b + 1)
            pe.wait_ge(s_("tp_free"), n * BLKS + b + 1)
            for k in range(2):
                for j in range(TPB):
                    last = nc.tensor.transpose(ps[0:KC, 2 * u + k, j * P:(j + 1) * P],
                                               xn[:, u, j, k * KC:(k + 1) * KC], ident)
            last.then_inc(s_("xn_free"), 1)

        def ln_tensor(pe, n):
            with pe.Fori(0, 2) as turn:
                for u in range(2):
                    ln_transpose(pe, n, turn * 2 + u, u)

        def ln_scalar(act, n):
            for turn in range(2):
                act.wait_ge(s_("ln_eps"), n * 2 + turn + 1)
                nc.scalar.activation(rstd[:], veps[:], ACT.Sqrt).then_inc(s_("ln_sqrt"), 1)
                for u in range(2):
                    b = turn * 2 + u
                    act.wait_ge(s_("xn_free"), n * BLKS + b + 1 + 2)
                    nc.scalar.activation(xnT_v[:, :, b * BT:(b + 1) * BT], ps[0:KC, 2 * u:2 * u + 2, :], ACT.Copy)\
                        .then_inc(s_("tp_free"), 1)

        def xnT_at(n, b):
            return n * BLKS + b + 3

        def perm_out(dst, i):
            n0 = 2 * WA + i * NB1
            return (dst[:, :, i * WA:(i + 1) * WA].rearrange("p b (y x) -> p b y x", x=WS),
                    dst[:, :, n0:n0 + NBD].rearrange("p b (y x) -> p b y x", x=SIDE - WS),
                    dst[:, :, n0 + NBD:n0 + NB1].rearrange("p b (y x) -> p b y x", x=WS))

        def perm_in(src, i):
            return (src[:, :, i, 0:WS, 0:WS], src[:, :, i, :, WS:SIDE], src[:, :, i, WS:SIDE, 0:WS])

        def permute(dst, src, rows):
            d = dst[0:rows].rearrange("p (b n) -> p b n", b=BLKS)
            s = blocks_of(src[0:rows])
            for i in range(2):
                for o, n in zip(perm_out(d, i), perm_in(s, i)):
                    last = nc.vector.tensor_copy(o, n)
            return last


        ST_A, ST_B, SM_A, SM_B, PV, MISC = 0, 2, 3, 5, 6, 7
        TR0_, R1_, TR1_, PA_, PB_, V1_, TR2_, R0_, TR3_, V0_ = range(10)
        AHEAD = 3

        def tr_use(blk, cc, first):
            return blk * 10 + ((AHEAD, AHEAD + 1, TR2_, TR3_) if first else (TR0_, TR1_, TR2_, TR3_))[cc]

        def peeled(eng, body):
            body(0, True, False)
            with eng.Fori(1, BLKS - 1) as blk:
                body(blk, False, False)
            body(BLKS - 1, False, True)

        def attn0_sync(sp):
            def load(blk, cc):
                f, g, hs = fq[cc % 2], fk[cc % 2], slice(cc * HC, (cc + 1) * HC)
                cols = bass.ds(blk * BT, BT)
                for r, lo, hi in ((0, 0, 32), (R_DUP, 0, HD), (R_REL2, 2 * HD, QROWS), (R_LO, 0, QROWS)):
                    sp.dma_start(f[r:r + hi - lo], qd[hs, lo:hi, cols].rearrange("h c n -> c h n"))\
                        .then_inc(s_(f"fq_in{cc % 2}"), 16)
                for r in (R_HI, R_DUP, R_LO):
                    sp.dma_start(g[r:r + HD], kd[hs, :, cols].rearrange("h c n -> c h n"))\
                        .then_inc(s_(f"fk_in{cc % 2}"), 16)

            def minus_max(n, cc):
                sp.wait_ge(s_("misc_free"), n + 1)
                sp.dma_start(q0[R_MAX:R_MAX + 1, cc].bitcast(F32), nm[0:HC, cc % 2, :].bitcast(F32))\
                    .then_inc(s_(f"nm_in{cc % 2}"), 16)

            sp.wait_ge(s_("pk_ready"), 1)
            sp.wait_ge(s_("fq_zero"), 1)
            for u in range(2):
                sp.dma_start(fk[u], a["ck"].unsqueeze(1).broadcast_to([P, HC, BT])).then_inc(s_("fk_rows"), 16)
            sp.wait_ge(s_("fk_rows"), 32)
            for c in range(CPB):
                if c >= 2:
                    sp.wait_ge(s_("q_lo"), c - 1)
                    sp.wait_ge(s_("k_lo"), c - 1)
                load(0, c)
            minus_max(2, 0)

            def body(blk, first, last):
                for cc in range(CPB):
                    chunk = blk * CPB + cc
                    if not (last and cc == 3):
                        minus_max(tr_use(blk, cc, first), (cc + 1) % CPB)
                    if not last:
                        sp.wait_ge(s_("q_lo"), chunk + 3)
                        sp.wait_ge(s_("k_lo"), chunk + 3)
                        load(blk + 1, cc)

            peeled(sp, body)

        def attn0_pool(pool):
            def window_order(blk, lows):
                pool.wait_ge(s_("k_lo"), lows)
                s = xnT_v[:, :, bass.ds(blk * BT, BT)].rearrange("p k (i y x) -> p k i y x", i=2, y=SIDE)
                for i in range(2):
                    for o, n in zip(perm_out(xp, i), perm_in(s, i)):
                        last = nc.gpsimd.tensor_copy(o, n)
                last.then_inc(s_("xp_ready"), 1)

            def k_low(chunk, cc, orders):
                pool.wait_ge(s_("xp_ready"), orders)
                pool.wait_ge(s_("k_lo"), chunk)
                pool.wait_ge(s_("k_rnd"), chunk + 1)
                dst = k0[R_DUP:R_DUP + HD, cc]
                nc.gpsimd.tensor_tensor(dst, fk[cc % 2][R_DUP:R_DUP + HD], dst.bitcast(F32), ALU.subtract)\
                    .then_inc(s_("k_lo"), 1)

            pool.wait_ge(s_("xn_ready"), BLKS)
            pool.wait_ge(s_("small_in"), 16 * 11)
            for b in range(BLKS):
                xs = x_sb[:, b * TPB:(b + 1) * TPB, :]
                nc.gpsimd.tensor_tensor(xs, xs, bp[0][:].unsqueeze(1).broadcast_to([P, TPB, C]), ALU.add)\
                    .then_inc(s_("x_bias"), 1)
            pool.wait_ge(s_("x_bias"), BLKS)
            pool.wait_ge(s_("rel_out"), 16)
            pool.wait_ge(s_("tp_free"), xnT_at(0, BLKS - 1))
            window_order(0, 0)
            for c in range(3):
                k_low(c, c, 1)

            def body(blk, first, last):
                for cc in range(CPB):
                    if not (last and cc >= 1):
                        k_low(blk * CPB + cc + 3, (cc + 3) % CPB, blk + 1 + (cc > 1))
                    if cc == 1 and not last:
                        pool.wait_ge(s_("misc_full"), blk * 10 + V1_ + 1)
                        window_order(blk + 1, blk * CPB + 5)

            peeled(pool, body)

        def attn0_vector(v):
            def maxima(chunk, cc, j):
                v.wait_ge(s_("sm_done"), chunk * HC + j + 1)
                nc.vector.tensor_reduce(mxa[0:WAH, cc % 2, :, j],
                                        ps[0:WAH, SM_A:SM_A + 2, 0:2 * WA].rearrange("p i (q n) -> p i q n", q=2),
                                        AX.X, ALU.max)
                nc.vector.tensor_reduce(mxb[0:NB, cc % 2, j:j + 1], ps[0:NB, SM_B, 0:NB + PADS], AX.X, ALU.max)\
                    .then_inc(s_("max_done"), 1)

            def minus(n, chunk, cc):
                v.wait_ge(s_("misc_full"), n + 1)
                nc.vector.tensor_scalar(nm[0:HC, cc % 2, :], ps[0:HC, MISC, :], -1.0, None, ALU.mult)\
                    .then_inc(s_("misc_free"), 1)

            def q_low(chunk, cc):
                v.wait_ge(s_("q_rnd"), chunk + 1)
                dst = q0[R_LO:R_ROUND, cc]
                nc.vector.tensor_tensor(dst, fq[cc % 2][R_LO:R_ROUND], dst.bitcast(F32), ALU.subtract)\
                    .then_inc(s_("q_lo"), 1)

            def values(n, g):
                v.wait_ge(s_("misc_full"), n + 1)
                bias = bv0[:].rearrange("p (g h c) -> p g h c", g=2, c=HD)
                for k in range(5):
                    rows = NB if k == 4 else WAH
                    dst = v0[0:rows, g, k, :].rearrange("p (h n) -> p h n", h=HG)[:, :, 0:HD]
                    src = ps[0:rows, MISC, k * KC:(k + 1) * KC].rearrange("p (h c) -> p h c", c=HD)
                    last = nc.vector.tensor_tensor(dst, src, bias[0:rows, g], ALU.add)
                last.then_inc(s_("misc_free"), 1)

            def reciprocals(group):
                v.wait_ge(s_("os_ready"), group + 1)
                nc.vector.reciprocal(osb[KC:KC + HG], osb[KC:KC + HG]).then_inc(s_("rc_ready"), 1)

            def normalise(n, group, g):
                v.wait_ge(s_("misc_full"), n + 1)
                o4 = ot[:, g, :].rearrange("p (i y x) -> p i y x", i=2, y=SIDE)
                parts = [o4[:, :, 0:WS, 0:WS], o4[:, :, :, WS:SIDE], o4[:, :, WS:SIDE, 0:WS]]
                n0 = 2 * WA

                def cut(s):
                    rest = s[:, n0:BT].rearrange("p (i n) -> p i n", i=2)
                    return (s[:, 0:n0].rearrange("p (i y x) -> p i y x", i=2, x=WS),
                            rest[:, :, 0:NBD].rearrange("p i (y x) -> p i y x", x=SIDE - WS),
                            rest[:, :, NBD:NB1].rearrange("p i (y x) -> p i y x", x=WS))

                for o, s, r in zip(parts, cut(osb[0:KC]), cut(ps[0:KC, MISC, :])):
                    last = nc.vector.tensor_tensor(o, s, r, ALU.mult)
                last.then_inc(s_("misc_free"), 1)

            def residual(n, blk, half):
                v.wait_ge(s_("misc_full"), n + 1)
                xs = x_sb[:, bass.ds(blk * TPB + 2 * half, 2), :]
                nc.vector.tensor_tensor(xs, xs, ps[:, MISC, 0:2 * C].rearrange("p (t c) -> p t c", t=2), ALU.add)\
                    .then_inc(s_("misc_free"), 1)

            for k in range(5, 8):
                v.wait_ge(s_(f"stored{k}"), 16)
            for u in range(2):
                last = nc.vector.memset(fq[u][32:64], 0.0)
            last.then_inc(s_("fq_zero"), 1)
            v.wait_ge(s_("rel_out"), 16)
            nc.vector.memset(v0, 0.0)
            nc.vector.memset(vpad, 0.0).then_inc(s_("v_zero"), 1)
            v.wait_ge(s_("v_zero"), 1)
            v.wait_ge(s_("small_in"), 16 * 11)
            nc.vector.tensor_copy(vpad.rearrange("p g (h n) -> p g h n", h=HG)[:, :, :, 0:HD],
                                  bv0[:].rearrange("p (g h c) -> p g h c", g=2, c=HD))
            for h in range(HG):
                at = h * VW + HG * HD + h
                nc.vector.memset(v0[:, :, :, at:at + 1], 1.0)
                last = nc.vector.memset(vpad[0:NB, :, at:at + 1], 1.0)
            last.then_inc(s_("v_ones"), 1)
            values(1, 0)
            for c in range(3):
                q_low(c, c)
            for c in range(2):
                for j in range(HC):
                    maxima(c, c, j)
                if c == 0:
                    minus(2, 0, 0)
            v.wait_ge(s_("x_bias"), BLKS)

            def body(blk, first, last):
                use = blk * 10
                for cc in range(CPB):
                    chunk = blk * CPB + cc
                    for j in range(HC):
                        if not (last and cc >= 2):
                            maxima(chunk + 2, (cc + 2) % CPB, j)
                        if (cc, j) == (0, 0) and not first:
                            reciprocals(blk * 2 - 1)
                        if (cc, j) == (2, 0):
                            reciprocals(blk * 2)
                        if j == 0 and not (last and cc == 3):
                            minus(tr_use(blk, cc, first), chunk + 1, (cc + 1) % CPB)
                        if j == 1 and not (last and cc >= 1):
                            q_low(chunk + 3, (cc + 3) % CPB)
                        if (cc, j) == (0, 2) and not first:
                            normalise(use + R1_, blk * 2 - 1, 1)
                        if (cc, j) == (1, 0) and not first:
                            residual(use + PA_, blk - 1, 0)
                            residual(use + PB_, blk - 1, 1)
                        if (cc, j) == (1, 1):
                            values(use + V1_, 1)
                        if (cc, j) == (2, 2):
                            normalise(use + R0_, blk * 2, 0)
                        if (cc, j) == (3, 1) and not last:
                            values(use + V0_, 0)

            peeled(v, body)
            reciprocals(2 * BLKS - 1)
            use = BLKS * 10 - 2
            normalise(use, 2 * BLKS - 1, 1)
            residual(use + 1, BLKS - 1, 0)
            residual(use + 2, BLKS - 1, 1)

        def attn0_tensor(pe):
            mm = nc.tensor.matmul

            def scores_for_max(chunk, cc, j):
                if j == 0:
                    pe.wait_ge(s_("q_lo"), chunk + 1)
                    pe.wait_ge(s_("k_lo"), chunk + 1)
                pe.wait_ge(s_("max_done"), chunk * HC + j)
                q, k, p_ = q0[0:K_MAX, cc, j], k0[0:K_MAX, cc, j], pk[0:K_MAX, cc * HC + j]
                for i in range(2):
                    for c in range(2):
                        at = i * WA + c * WAH
                        mm(ps[0:WAH, SM_A + i, c * WA:(c + 1) * WA], q[:, at:at + WAH], k[:, i * WA:(i + 1) * WA],
                           start=True, stop=True)
                mm(ps[0:NB, SM_B, 0:NB], q[:, 2 * WA:BT], k[:, 2 * WA:BT], start=True, stop=True)
                mm(ps[0:NB, SM_B, NB:NB + PADS], q[:, 2 * WA:BT], p_, start=True, stop=True).then_inc(s_("sm_done"), 1)

            def scores(blk, cc, j):
                chunk = blk * CPB + cc
                if j == 0:
                    pe.wait_ge(s_(f"nm_in{cc % 2}"), (blk * 2 + cc // 2 + 1) * 16)
                pe.wait_ge(s_("exp_done"), chunk * HC + j)
                q, k, p_ = q0[0:R_MAX + 1, cc, j], k0[0:R_MAX + 1, cc, j], pk[0:R_MAX + 1, cc * HC + j]
                for i in range(2):
                    for c in range(2):
                        at = i * WA + c * WAH
                        mm(ps[0:WAH, ST_A + i, c * WA:(c + 1) * WA], k[:, at:at + WAH], q[:, i * WA:(i + 1) * WA],
                           start=True, stop=True)
                rhs = q[:, 2 * WA:BT]
                mm(ps[0:NB, ST_B, 0:NB], k[:, 2 * WA:BT], rhs, start=True, stop=True)
                for c in range(2):
                    last = mm(ps[0:NB, ST_B, (c + 1) * NB:(c + 2) * NB], p_[:, c * NB:(c + 1) * NB], rhs,
                              start=True, stop=True)
                last.then_inc(s_("st_done"), 1)

            def values_product(blk, cc, j):
                h = cc * HC + j
                n = blk * NH + h
                if cc % 2 == 0 and j == 0:
                    pe.wait_ge(s_("os_ready"), blk * 2 + cc // 2)
                pe.wait_ge(s_("exp_done"), n + 1)
                g, hh = h // HG, h % HG
                at = slice(hh * VW, (hh + 1) * VW)
                x, y = pa[h % 2], pb[h % 2]
                first = hh == 0
                for i in range(2):
                    for c in range(2):
                        mm(ps[0:VW, PV, i * WA:(i + 1) * WA], v0[0:WAH, g, 2 * i + c, at],
                           x[0:WAH, i, c * WA:(c + 1) * WA], start=first, stop=False, skip_group_check=True)
                        first = False
                for c in range(3):
                    vs = v0[0:NB, g, 4, at] if c == 0 else vpad[0:NB, g, at]
                    last = mm(ps[0:VW, PV, 2 * WA:BT], vs, y[0:NB, c], start=False, stop=hh == HG - 1 and c == 2,
                              skip_group_check=True)
                last.then_inc(s_("pv_done"), 1)

            def transposed_maxima(n, chunk, cc):
                pe.wait_ge(s_("misc_free"), n)
                pe.wait_ge(s_("max_done"), chunk * HC + HC)
                for k in range(4):
                    nc.tensor.transpose(ps[0:HC, MISC, k * WAH:(k + 1) * WAH], mxa[0:WAH, cc % 2, k, :],
                                        ident[0:WAH, 0:WAH])
                nc.tensor.transpose(ps[0:HC, MISC, 2 * WA:BT], mxb[0:NB, cc % 2, :], ident[0:NB, 0:NB])\
                    .then_inc(s_("misc_full"), 1)

            def values(n, blk, g):
                pe.wait_ge(s_("misc_free"), n)
                pe.wait_ge(s_("xp_ready"), blk + 1)
                for k in range(5):
                    rows = NB if k == 4 else WAH
                    for kc in range(2):
                        last = mm(ps[0:rows, MISC, k * KC:(k + 1) * KC], xp[:, kc, k * WAH:k * WAH + rows],
                                  wv0[:, kc, g * KC:(g + 1) * KC], start=kc == 0, stop=kc == 1)
                last.then_inc(s_("misc_full"), 1)

            def spread_reciprocals(n, group):
                pe.wait_ge(s_("misc_free"), n)
                pe.wait_ge(s_("rc_ready"), group + 1)
                mm(ps[0:KC, MISC, :], CST["sel"][KC:KC + HG, :], osb[KC:KC + HG], start=True, stop=True)\
                    .then_inc(s_("misc_full"), 1)

            def projection(n, half):
                pe.wait_ge(s_("misc_free"), n)
                for u in range(2):
                    at = (2 * half + u) * P
                    for k in range(2):
                        last = mm(ps[:, MISC, u * C:(u + 1) * C], ot[:, k, at:at + P], wp[0][:, k, :],
                                  start=k == 0, stop=k == 1)
                last.then_inc(s_("misc_full"), 1)

            pe.wait_ge(s_("v_ones"), 1)
            pe.wait_ge(s_("rows_set"), 2)
            pe.wait_ge(s_("pk_ready"), 1)
            values(1, 0, 0)
            for c in range(2):
                for j in range(HC):
                    scores_for_max(c, c, j)
                if c == 0:
                    transposed_maxima(2, 0, 0)

            def body(blk, first, last):
                use = blk * 10
                for cc in range(CPB):
                    chunk = blk * CPB + cc
                    for j in range(HC):
                        scores(blk, cc, j)
                        if not (last and cc >= 2):
                            scores_for_max(chunk + 2, (cc + 2) % CPB, j)
                        if cc or j:
                            values_product(blk, cc - (j == 0), (j - 1) % HC)
                        elif not first:
                            values_product(blk - 1, CPB - 1, HC - 1)
                        if j == 0 and not (last and cc == 3):
                            transposed_maxima(tr_use(blk, cc, first), chunk + 1, (cc + 1) % CPB)
                        if (cc, j) == (0, 2) and not first:
                            spread_reciprocals(use + R1_, blk * 2 - 1)
                        if (cc, j) == (1, 0) and not first:
                            projection(use + PA_, 0)
                            projection(use + PB_, 1)
                        if (cc, j) == (1, 1):
                            values(use + V1_, blk, 1)
                        if (cc, j) == (2, 2):
                            spread_reciprocals(use + R0_, blk * 2)
                        if (cc, j) == (3, 1) and not last:
                            values(use + V0_, blk + 1, 0)

            peeled(pe, body)
            values_product(BLKS - 1, CPB - 1, HC - 1)
            use = BLKS * 10 - 2
            spread_reciprocals(use, 2 * BLKS - 1)
            projection(use + 1, 0)
            projection(use + 2, 1)

        def attn0_scalar(act):
            def exponentials(blk, cc, j):
                h = cc * HC + j
                n = blk * NH + h
                act.wait_ge(s_("st_done"), n + 1)
                act.wait_ge(s_("pv_done"), n)
                nc.scalar.activation(pa[h % 2][0:WAH], ps[0:WAH, ST_A:ST_A + 2, 0:2 * WA], ACT.Exp)
                nc.scalar.activation(pb[h % 2][0:NB], ps[0:NB, ST_B, 0:3 * NB].rearrange("p (c n) -> p c n", c=3), ACT.Exp)\
                    .then_inc(s_("exp_done"), 1)

            def round_q(blk, n):
                cc = n % CPB
                act.wait_ge(s_(f"fq_in{n % 2}"), (blk * 2 + n // 2 + 1) * 64)
                nc.scalar.activation(q0[0:R_ROUND, cc], fq[cc % 2][0:R_ROUND], ACT.Copy).then_inc(s_("q_rnd"), 1)

            def round_k(blk, n):
                cc = n % CPB
                act.wait_ge(s_(f"fk_in{n % 2}"), (blk * 2 + n // 2 + 1) * 48)
                nc.scalar.activation(k0[0:R_ROUND, cc], fk[cc % 2][0:R_ROUND], ACT.Copy).then_inc(s_("k_rnd"), 1)

            def unnormalised(group, last_read):
                act.wait_ge(s_("misc_free"), last_read + 1)
                act.wait_ge(s_("pv_done"), group * HG + HG + 1)
                nc.scalar.activation(osb[0:VW], ps[0:VW, PV, :], ACT.Copy).then_inc(s_("os_ready"), 1)

            for c in range(3):
                round_q(0, c)
                round_k(0, c)

            def body(blk, first, last):
                for cc in range(CPB):
                    chunk = blk * CPB + cc
                    for j in range(HC):
                        exponentials(blk, cc, j)
                        ahead = not (last and cc >= 1)
                        if (cc, j) == (0, 0) and not first:
                            unnormalised(blk * 2 - 1, (blk - 1) * 10 + R0_)
                        if (cc, j) == (2, 0):
                            unnormalised(blk * 2, blk * 10 + R1_)
                        if j == 0 and ahead:
                            round_q(blk, cc + 3)
                        if j == 1 and ahead:
                            round_k(blk, cc + 3)

            peeled(act, body)
            unnormalised(2 * BLKS - 1, (BLKS - 1) * 10 + R0_)

        LOGITS, RANKS, TOTALS, TABLES = 4, 5, 6, 7
        DOWN, XT = 6, 7
        TRIPS = MT // 3
        COLS = 2 * TILES

        def tripled(eng, body):
            for r in range(3):
                body(0, r, r == 0, False)
            with eng.Fori(1, TRIPS - 1) as trip:
                for r in range(3):
                    body(trip, r, False, False)
            for r in range(3):
                body(TRIPS - 1, r, False, True)

        def moe_sync(sp, l):
            if l == 0:
                sp.wait_ge(s_("misc_free"), 10 * BLKS + 1)
            else:
                sp.wait_ge(s_("y1_out"), 16 * 4 * len(DIL))
            for e in range(E):
                if e in (2, 4):
                    for u in range(2):
                        sp.wait_ge(s_(f"xn_kept{u}"), 16 * (2 * l + e // 2))
                sp.dma_start(w1s[:, e], a[f"w1_{l}"][e]).then_inc(s_("w_in"), 16)
                sp.dma_start(w2s[:, e], a[f"w2_{l}"][e]).then_inc(s_("w_in"), 16)
            for u in range(2):
                sp.wait_ge(s_(f"xn_kept{u}"), 16 * 2 * (l + 1))
            sp.wait_ge(s_("xn_free"), 2 + (2 + 2 * l) * BLKS)
            sp.dma_start(b2s.rearrange("p e c -> p (e c)"), a[f"b2_{l}"]).then_inc(s_("w_in"), 16)
            for r in range(3):
                sp.wait_ge(s_(f"scattered{r}"), 16 * TRIPS * (l + 1))
            for b in range(BLKS):
                sp.dma_start(yt[:, b * TPB:(b + 1) * TPB],
                             yd[l].rearrange("(t p k) c -> p t k c", p=P, k=2)[:, b * TPB:(b + 1) * TPB])\
                    .then_inc(s_(f"y_in{b}"), 16)

        def moe_vector(v, l):
            vec = nc.vector
            at = [0]

            def tmp(*shape):
                n = 1
                for s in shape:
                    n *= s
                view = rt[:, at[0]:at[0] + n]
                at[0] += n
                if len(shape) > 1:
                    names = "abcd"[:len(shape)]
                    view = view.rearrange(f"p ({' '.join(names)}) -> p {' '.join(names)}",
                                          **dict(zip(names, shape)))
                return view

            logits, masked, shifted, place, ex = (tmp(TILES, E) for _ in range(5))
            hot = tmp(2, TILES, E)
            top, second, best, total, share = (tmp(TILES) for _ in range(5))
            scan = [tmp(COLS, E) for _ in range(2)]
            slot = tmp(COLS, E)
            counts, tiles, first_tile, base, end = (tmp(E) for _ in range(5))
            below = tmp(E, E)
            pos, row, tile_ = tmp(COLS), tmp(COLS), tmp(COLS)
            low, table, empty = tmp(SLOTS), tmp(SLOTS), tmp(SLOTS)
            over = tmp(SLOTS, E)
            hot_flat = hot.rearrange("p k t e -> p (k t) e")
            rowb = smallb[:, 0:COLS]
            tileb = smallb[:, COLS:2 * COLS]
            rowhot = xnT[:, 0:COLS * P // 2].bitcast(BF16).rearrange("p (c n) -> p c n", c=COLS)
            ids = xnT[:, 2048:2048 + COLS * SLOTS].bitcast(BF16).rearrange("p (c k s) -> p c k s", c=COLS, k=2)
            tilehot = xnT[:, 3392:3392 + COLS * SLOTS // 2].bitcast(BF16).rearrange("p (c s) -> p c s", c=COLS)
            count = [l * ROUTE_STEPS[0]]

            def step(instruction):
                instruction.then_inc(s_("route"), 1)
                count[0] += 1
                v.wait_ge(s_("route"), count[0])

            def per_token(x):
                return x.unsqueeze(2).broadcast_to([P, TILES, E])

            def per_column(x):
                return x.unsqueeze(1).broadcast_to([P, COLS, E])

            rev = CST["rev"].unsqueeze(1).broadcast_to([P, TILES, E])
            ln_vector(v, 1 + 2 * l)
            v.wait_ge(s_("logits_mm"), (l + 1) * BLKS)
            step(vec.tensor_tensor(logits, ps[:, LOGITS, 0:TILES * E].rearrange("p (t e) -> p t e", e=E),
                                   bg[l][:].unsqueeze(1).broadcast_to([P, TILES, E]), ALU.add))
            for k, (src, value) in enumerate(((logits, top), (masked, second))):
                step(vec.tensor_reduce(value, src, AX.X, ALU.max))
                step(vec.tensor_tensor(place, src, per_token(value), ALU.is_equal))
                step(vec.tensor_tensor(place, place, rev, ALU.mult))
                step(vec.tensor_reduce(best, place, AX.X, ALU.max))
                step(vec.tensor_tensor(hot[:, k], place, per_token(best), ALU.is_equal))
                if k == 0:
                    vec.tensor_tensor(shifted, logits, per_token(top), ALU.subtract).then_inc(s_("shifted"), 1)
                    step(vec.scalar_tensor_tensor(masked, hot[:, 0], -1e30, logits, ALU.mult, ALU.add))
            vec.tensor_copy(hotb_v, hot_flat).then_inc(s_("hot_ready"), 1)
            v.wait_ge(s_("exp_gates"), l + 1)
            step(vec.tensor_reduce(total, ex, AX.X, ALU.add))
            step(vec.reciprocal(gw[:, 0], total))
            step(vec.tensor_tensor(place, ex, hot[:, 1], ALU.mult))
            step(vec.tensor_reduce(share, place, AX.X, ALU.add))
            step(vec.tensor_tensor(gw[:, 1], share, gw[:, 0], ALU.mult))
            if l == 1:
                step(vec.tensor_tensor(total, gw[:, 0], gw[:, 1], ALU.add))
                step(vec.tensor_scalar(total, total, 1e-9, None, ALU.add))
                step(vec.reciprocal(total, total))
                step(vec.tensor_tensor(gw[:], gw[:], total.unsqueeze(1).broadcast_to([P, 2, TILES]), ALU.mult))
            v.wait_ge(s_("ranks_mm"), l + 1)
            totals = ps[:, TOTALS, 0:COLS * E].rearrange("p (c e) -> p c e", e=E)
            step(vec.tensor_copy(scan[0], totals))
            d, cur = 1, 0
            while d < COLS:
                vec.tensor_copy(scan[1 - cur][:, 0:d], scan[cur][:, 0:d])
                step(vec.tensor_tensor(scan[1 - cur][:, d:], scan[cur][:, d:], scan[cur][:, 0:COLS - d], ALU.add))
                d, cur = 2 * d, 1 - cur
            sums = scan[cur]
            step(vec.tensor_tensor(slot, sums, totals, ALU.subtract))
            step(vec.tensor_tensor(slot, slot, ps[:, RANKS, 0:COLS * E].rearrange("p (c e) -> p c e", e=E), ALU.add))
            step(vec.tensor_scalar(counts.bitcast(I32), sums[:, COLS - 1], float(P - 1), None, ALU.add))
            step(vec.tensor_scalar(counts.bitcast(I32), counts.bitcast(I32), 7, None, ALU.logical_shift_right))
            step(vec.tensor_copy(tiles, counts.bitcast(I32)))
            step(vec.tensor_tensor(below, CST["lt"].rearrange("p (a b) -> p a b", a=E),
                                   tiles.unsqueeze(1).broadcast_to([P, E, E]), ALU.mult))
            step(vec.tensor_reduce(first_tile, below, AX.X, ALU.add))
            vec.tensor_scalar(base, first_tile, float(P), None, ALU.mult)
            step(vec.tensor_tensor(end, first_tile, tiles, ALU.add))
            step(vec.tensor_tensor(slot, slot, per_column(base), ALU.add))
            step(vec.tensor_tensor(slot, slot, hot_flat, ALU.mult))
            step(vec.tensor_reduce(pos, slot, AX.X, ALU.add))
            vec.tensor_copy(row.bitcast(I32), pos)
            step(vec.tensor_tensor(over[0:1], CST["iots"][0:1].unsqueeze(2).broadcast_to([1, SLOTS, E]),
                                   end[0:1].unsqueeze(1).broadcast_to([1, SLOTS, E]), ALU.is_ge))
            step(vec.tensor_reduce(low[0:1], over[0:1], AX.X, ALU.add))
            vec.tensor_scalar(te[:], low[0:1], float(E - 1), None, ALU.min).then_inc(s_("te_ready"), 1)
            vec.tensor_scalar(tile_.bitcast(I32), row.bitcast(I32), 7, None, ALU.logical_shift_right)
            step(vec.tensor_scalar(pos.bitcast(I32), row.bitcast(I32), P - 1, None, ALU.bitwise_and))
            vec.tensor_copy(rowb, pos.bitcast(I32))
            step(vec.tensor_copy(tileb, tile_.bitcast(I32)))
            vec.tensor_tensor(rowhot, iotb.unsqueeze(1).broadcast_to([P, COLS, P]),
                              rowb.unsqueeze(2).broadcast_to([P, COLS, P]), ALU.is_equal)
            step(vec.tensor_tensor(tilehot, iotsb.unsqueeze(1).broadcast_to([P, COLS, SLOTS]),
                                   tileb.unsqueeze(2).broadcast_to([P, COLS, SLOTS]), ALU.is_equal))
            for k, name in enumerate((idab, idbb)):
                last = vec.tensor_tensor(ids[:, :, k], tilehot, name.unsqueeze(2).broadcast_to([P, COLS, SLOTS]),
                                         ALU.mult)
            last.then_inc(s_("ids_ready"), 1)
            v.wait_ge(s_("tables_mm"), l + 1)
            step(vec.tensor_copy(low, ps[:, TABLES, SLOTS:2 * SLOTS]))
            step(vec.scalar_tensor_tensor(table, ps[:, TABLES, 0:SLOTS], 64.0, low, ALU.mult, ALU.add))
            step(vec.tensor_scalar(empty, table, 0.0, 4.0 * T, ALU.is_equal, ALU.mult))
            vec.tensor_scalar(low.bitcast(I32), table, -1.0, 0.0, ALU.add, ALU.max)
            step(vec.tensor_scalar(table, table, -1.0, None, ALU.add))
            step(vec.tensor_tensor(sidx[:], table, empty, ALU.add))
            vec.memset(xgT[KC:KC + 1, 0], 1.0)
            step(vec.tensor_scalar(gidx[:], low.bitcast(I32), 1, None, ALU.logical_shift_right))
            vec.memset(credit[0:1, 7:8], 0.0).then_inc(s_("routed"), 1)
            ROUTE_STEPS[0] = count[0] if l == 0 else ROUTE_STEPS[0]

            n0 = l * MT

            def gathered(n):
                v.wait_ge(s_("trx_done"), n + 1)
                vec.tensor_copy(xgT[0:KC], ps[0:KC, XT, 0:2 * P].rearrange("p (k n) -> p k n", k=2))\
                    .then_inc(s_("xgT_ready"), 1)

            def result(n, trip, r):
                e = v.value_load(te[0:1, bass.ds(n - n0, 1)], min_val=0, max_val=E - 1)
                v.wait_ge(s_("down_done"), n + 1)
                v.wait_ge(s_(f"scattered{r}"), (trip + l * TRIPS) * 16)
                vec.tensor_tensor(ys[r], ps[:, DOWN, 0:C], b2s[:, e, :], ALU.add).then_inc(s_("y_ready"), 1)

            def expert_weights(n, trip, r, wait=True):
                e = v.value_load(te[0:1, bass.ds(n - n0, 1)], min_val=0, max_val=E - 1)
                if wait:
                    v.wait_ge(s_("up_done"), n - 2)
                for k in range(2):
                    last = vec.tensor_copy(wcur[r][k][0:KC + 1 - k], w1s[0:KC + 1 - k, e, k, :])
                last.then_inc(s_("wcur_ready"), 1)

            def body(trip, r, first, last):
                n = n0 + trip * 3 + r
                if not (last and r >= 1):
                    expert_weights(n + 2, trip + (r > 0), (r + 2) % 3, not (first and r == 0))
                if not (last and r == 2):
                    gathered(n + 1)
                if not (first and r == 0):
                    result(n - 1, trip - (r == 0), (r - 1) % 3)

            v.wait_ge(s_("w_in"), 16 * 17 * (l + 1))
            for r in range(2):
                expert_weights(n0 + r, 0, r, False)
            gathered(n0)
            tripled(v, body)
            result(n0 + MT - 1, TRIPS - 1, 2)
            for b in range(BLKS):
                v.wait_ge(s_(f"y_in{b}"), 16 * (l + 1))
                for k in range(2):
                    if k:
                        v.wait_ge(s_("first_added"), l * BLKS + b + 1)
                    for t in range(b * TPB, (b + 1) * TPB):
                        last = vec.scalar_tensor_tensor(x_sb[:, t], yt[:, t, k], gw[:, k, t:t + 1], x_sb[:, t],
                                                        ALU.mult, ALU.add)
                    last.then_inc(s_("combined" if k else "first_added"), 1)
            if l == 0:
                v.wait_ge(s_("combined"), BLKS)

        def moe_tensor(pe, l):
            n0 = l * MT
            mm = nc.tensor.matmul
            def logits(b):
                pe.wait_ge(s_("tp_free"), xnT_at(1 + 2 * l, b))
                for t in range(b * TPB, (b + 1) * TPB):
                    for k in range(2):
                        last = mm(ps[:, LOGITS, t * E:(t + 1) * E], xnT_v[:, k, t * P:(t + 1) * P], wg[l][:, k, :],
                                  start=k == 0, stop=k == 1)
                last.then_inc(s_("logits_mm"), 1)

            for b in range(BLKS):
                ln_transpose(pe, 1 + 2 * l, b, b % 2)
                if b:
                    logits(b - 1)
            logits(BLKS - 1)
            pe.wait_ge(s_("hot_ready"), l + 1)
            flat = hotb_v.rearrange("p c e -> p (c e)")
            mm(ps[:, RANKS, 0:COLS * E], trib, flat, start=True, stop=True)
            mm(ps[:, TOTALS, 0:COLS * E], onesb, flat, start=True, stop=True).then_inc(s_("ranks_mm"), 1)
            pe.wait_ge(s_("ids_ready"), l + 1)
            rowhot = xnT[:, 0:COLS * P // 2].bitcast(BF16).rearrange("p (c n) -> p c n", c=COLS)
            ids = xnT[:, 2048:2048 + COLS * SLOTS].bitcast(BF16).rearrange("p (c n) -> p c n", c=COLS)
            for c in range(COLS):
                last = mm(ps[:, TABLES, 0:2 * SLOTS], rowhot[:, c], ids[:, c], start=c == 0, stop=c == COLS - 1)
            last.then_inc(s_("tables_mm"), 1)

            def gathered(n, trip, r):
                pe.wait_ge(s_(f"gathered{r}"), (trip + 1 + l * TRIPS) * 16)
                pe.wait_ge(s_("xgT_ready"), n)
                for k in range(2):
                    last = nc.tensor.transpose(ps[0:KC, XT, k * P:(k + 1) * P], xg[r][:, k * KC:(k + 1) * KC], ident)
                last.then_inc(s_("trx_done"), 1)

            def down(n):
                e = pe.value_load(te[0:1, bass.ds(n - n0, 1)], min_val=0, max_val=E - 1)
                pe.wait_ge(s_("hid_ready"), n + 1)
                pe.wait_ge(s_("y_ready"), n)
                for f in range(FT):
                    last = mm(ps[:, DOWN, 0:C], hidT[:, f, :], w2s[:, e, f, :], start=f == 0, stop=f == FT - 1)
                last.then_inc(s_("down_done"), 1)

            def body(trip, r, first, last_):
                n = n0 + trip * 3 + r
                pe.wait_ge(s_("xgT_ready"), n + 1)
                pe.wait_ge(s_("wcur_ready"), n + 1)
                for f in range(FT):
                    for k in range(2):
                        rows = KC + 1 - k
                        last = mm(ps[:, 2 * r + f // 4, f % 4 * P:(f % 4 + 1) * P],
                                  wcur[r][k][0:rows, f * P:(f + 1) * P], xgT[0:rows, k, :], start=k == 0, stop=k == 1)
                last.then_inc(s_("up_done"), 1)
                if not (last_ and r == 2):
                    gathered(n + 1, trip + (r == 2), (r + 1) % 3)
                if not (first and r == 0):
                    down(n - 1)

            pe.wait_ge(s_("w_in"), 16 * 17 * (l + 1))
            pe.wait_ge(s_("te_ready"), l + 1)
            gathered(n0, 0, 0)
            tripled(pe, body)
            down(n0 + MT - 1)

        def moe_scalar(act, l):
            banks = ps[:].rearrange("p b n -> p (b n)")
            ln_scalar(act, 1 + 2 * l)
            act.wait_ge(s_("shifted"), l + 1)
            nc.scalar.activation(rt[:, 4 * TILES * E:5 * TILES * E], rt[:, 2 * TILES * E:3 * TILES * E], ACT.Exp)\
                .then_inc(s_("exp_gates"), 1)

            def body(trip, r, first, last):
                n = l * MT + trip * 3 + r
                act.wait_ge(s_("up_done"), n + 1)
                act.wait_ge(s_("down_done"), n)
                nc.scalar.activation(hidT.rearrange("p f n -> p (f n)"), banks[:, 2 * r * 512:2 * r * 512 + F], ACT.Gelu)\
                    .then_inc(s_("hid_ready"), 1)

            tripled(act, body)

        def moe_pool(pool, l):
            def held(kind, before):
                pool.wait_ge(s_(f"held{kind}"), before)
                nc.gpsimd.tensor_tensor(credit[0:1, 12 + kind:13 + kind], credit[0:1, 0:1], credit[0:1, 0:1], ALU.add)\
                    .then_inc(s_(f"held{kind}"), 1)

            def gather(n, r):
                nc.gpsimd.tensor_copy(gcur[:, r:r + 1], gidx[:, bass.ds(n - n0, 1)]).then_inc(s_("gcur_ready"), 1)
                pool.wait_ge(s_("gcur_ready"), n + 1)
                held(1, n)
                nc.gpsimd.indirect_dma_start(out=xg[r], out_offset=None, in_=xnd[l],
                                             in_offset=bass.IndirectOffsetOnAxis(ap=gcur[:, r:r + 1], axis=0))\
                    .then_inc(s_(f"gathered{r}"), 16)

            def scatter(n, r):
                pool.wait_ge(s_("y_ready"), n + 1)
                held(2, n)
                nc.gpsimd.tensor_copy(scur[:, r:r + 1], sidx[:, bass.ds(n - n0, 1)]).then_inc(s_("scur_ready"), 1)
                pool.wait_ge(s_("scur_ready"), n + 1)
                held(3, n)
                nc.gpsimd.indirect_dma_start(out=yd[l], out_offset=bass.IndirectOffsetOnAxis(ap=scur[:, r:r + 1], axis=0),
                                             in_=ys[r], in_offset=None, bounds_check=2 * T - 1, oob_is_err=False)\
                    .then_inc(s_(f"scattered{r}"), 16)

            n0 = l * MT
            for b in range(BLKS):
                pool.wait_ge(s_("xn_ready"), (1 + 2 * l) * BLKS + b + 1)
                pool.dma_start(xnd[l][b * BT:(b + 1) * BT].rearrange("(t p) c -> p t c", p=P), xn[:, b % 2])\
                    .then_inc(s_(f"xn_kept{b % 2}"), 16)
            for u in range(2):
                pool.wait_ge(s_(f"xn_kept{u}"), 16 * 2 * (l + 1))
            pool.wait_ge(s_("routed"), l + 1)
            for r in range(3):
                gather(n0 + r, r)

            def body(trip, r, first, last):
                n = n0 + trip * 3 + r
                if not last:
                    pool.wait_ge(s_("trx_done"), n + 1)
                    held(0, n - l * 3)
                    gather(n + 3, r)
                if not first:
                    scatter(n - 1, (r - 1) % 3)

            tripled(pool, body)
            scatter(n0 + MT - 1, 2)

        QR = SIDE // 4
        QPIX = QR * SIDE
        NEIGH = [(dy, dx) for dx in (0, -1, 1) for dy in (-1, 0, 1)]
        NN = len(NEIGH)

        def halo(d):
            return QR + 2 * d

        def columns(d, dx):
            return max(0, -dx * d), SIDE - d * abs(dx)

        k1, v1 = [], []
        at1 = 0
        for views in (k1, v1):
            for d in DIL:
                views.append(ar(at1, [HD, halo(d), SIDE]))
                at1 += HD * halo(d) * SIDE
        halos = at1
        q1 = [ar(at1 + i * HD * QPIX, [HD, QR, SIDE]) for i in range(3)]
        at1 += 3 * HD * QPIX
        stage = [ar(at1 + u * 6 * BT, [2, 3, BT], KC) for u in range(2)]
        acc = [ar(at1 + i * QPIX * HD, [QPIX * HD]) for i in range(3)]
        prod = [xt_(u * HD * QPIX, [HD * QPIX]) for u in range(4)]
        yl = xt_(0, [TILES, C])
        sc = [rt[:, i * NN * QPIX:(i + 1) * NN * QPIX] for i in range(3)]
        mx1 = rt[:, 3 * NN * QPIX:3 * NN * QPIX + QPIX]
        sm1 = [rt[:, 3 * NN * QPIX + (1 + i) * QPIX:3 * NN * QPIX + (2 + i) * QPIX] for i in range(3)]
        yT = [rt[0:KC, u * 2 * BT:(u + 1) * 2 * BT].rearrange("p (k n) -> p k n", k=2) for u in range(2)]

        QKV_DMAS = GRP // 2 * 6

        def store_qkv(eng, i):
            for g in range(GRP):
                for u in range(6):
                    n = i * 36 + u * 6
                    eng.wait_ge(s_("qkv_staged"), g * 6 + u + 3)
                    eng.dma_start(qkvd[n:n + 6, g], stage[g % 2][:, u // 3, u % 3, i * PIX:(i + 1) * PIX])\
                        .then_inc(s_(f"qkv_out{i}{g % 2}"), 16)

        def attn1_sync(sp):
            store_qkv(sp, 0)
            for i in range(2):
                for u in range(2):
                    sp.wait_ge(s_(f"qkv_out{i}{u}"), 16 * QKV_DMAS)
            sp.wait_ge(s_("halo_zero"), 2)
            for i, d in enumerate(DIL):
                for t, name, dst in ((0, "qk", q1), (1, "qk", k1), (2, "v", v1)):
                    n = (i * 3 + t) * SPU
                    src = qkvd[n:n + SPU].rearrange("b g c x -> (b g) c x")
                    edge = d if t else 0
                    for quarter in range(4):
                        lo = max(0, quarter * QR - edge)
                        hi = min(SIDE, (quarter + 1) * QR + edge)
                        row = lo - (quarter * QR - edge)
                        to = dst[i][quarter * 32:(quarter + 1) * 32, :, row:row + hi - lo, :]
                        sp.dma_start(to.rearrange("p c y x -> p c (y x)"), src[:, :, lo * SIDE:hi * SIDE])\
                            .then_inc(s_(f"{name}_in{i}"), 16)
            for i in range(3):
                sp.wait_ge(s_("acc_ready"), i + 1)
                for quarter in range(4):
                    dst = y1d.rearrange("(g i b) (q n) c -> i q b g (n c)", i=3, b=SPU, q=4)[i, quarter]
                    sp.dma_start(dst, acc[i][quarter * 32:(quarter + 1) * 32]).then_inc(s_("y1_out"), 16)
            sp.wait_ge(s_("y1_out"), 16 * 12)
            flat = y1d.rearrange("s n c -> (s n c)").rearrange("(t p c) -> p t c", p=P, c=C)
            for b in range(BLKS):
                sp.dma_start(yl[:, b * TPB:(b + 1) * TPB], flat[:, b * TPB:(b + 1) * TPB])\
                    .then_inc(s_(f"yl_in{b}"), 16)

        def attn1_pool(pool):
            pool.wait_ge(s_("y_ready"), MT)
            nc.gpsimd.memset(ar(halos // 2, [halos // 2]), 0.0).then_inc(s_("halo_zero"), 1)
            pool.wait_ge(s_("combined"), BLKS)
            nc.gpsimd.memset(ar(0, [halos // 2]), 0.0).then_inc(s_("halo_zero"), 1)
            store_qkv(pool, 1)
            pool.wait_ge(s_("halo_zero"), 2)
            pool.wait_ge(s_("xn_ready"), 3 * BLKS)
            for b in range(BLKS):
                xs = x_sb[:, b * TPB:(b + 1) * TPB, :]
                nc.gpsimd.tensor_tensor(xs, xs, bp[1][:].unsqueeze(1).broadcast_to([P, TPB, C]), ALU.add)\
                    .then_inc(s_("x_bias"), 1)
            for i in range(3):
                pool.wait_ge(s_("norm"), 3 * (i + 1))
                value_products(pool, nc.gpsimd, i)

        def by_pool(i, n):
            return i < 2 or n % 3 == 2

        POOLS = [sum(by_pool(m // NN, m % NN) for m in range(k)) for k in range(3 * NN + 1)]

        def value_products(eng, ops, i):
            pool = ops is nc.gpsimd
            eng.wait_ge(s_(f"v_in{i}"), 4 * 16)
            for n, (dy, dx) in enumerate(NEIGH):
                if by_pool(i, n) != pool:
                    continue
                d, m = DIL[i], i * NN + n
                x0, w = columns(d, dx)
                if m >= 2:
                    eng.wait_ge(s_("pv_sum"), m - 1)
                o = prod[2 + m % 2].rearrange("p (y x c) -> p y x c", c=HD, x=SIDE)[:, :, x0:x0 + w, :]
                weight = sc[i][:, n * QPIX:(n + 1) * QPIX].rearrange("p (y x) -> p y x", x=SIDE)[:, :, x0:x0 + w]
                val = v1[i][:, :, d + dy * d:d + dy * d + QR, x0 + dx * d:x0 + dx * d + w]
                ops.tensor_tensor(o, val.rearrange("p c y x -> p y x c"),
                                  weight.unsqueeze(3).broadcast_to([P, QR, w, HD]), ALU.mult)\
                    .then_inc(s_("pv_pool" if pool else "pv_vector"), 1)

        def attn1_vector(v):
            ln_vector(v, 2)

            def product(i, n):
                d, (dy, dx) = DIL[i], NEIGH[n]
                x0, w = columns(d, dx)
                o = prod[n % 2].rearrange("p (c y x) -> p c y x", c=HD, x=SIDE)[:, :, :, x0:x0 + w]
                key = k1[i][:, :, d + dy * d:d + dy * d + QR, x0 + dx * d:x0 + dx * d + w]
                if n >= 2 or i:
                    v.wait_ge(s_("qk_sum"), i * NN + n - 1)
                nc.vector.tensor_tensor(o, q1[i][:, :, :, x0:x0 + w], key, ALU.mult).then_inc(s_("qk_prod"), 1)

            def channel_sum(i, n):
                x0, w = columns(DIL[i], NEIGH[n][1])
                src = prod[n % 2].rearrange("p (c y x) -> p y x c", c=HD, x=SIDE)[:, :, x0:x0 + w, :]
                o = sc[i][:, n * QPIX:(n + 1) * QPIX].rearrange("p (y x) -> p y x", x=SIDE)[:, :, x0:x0 + w]
                v.wait_ge(s_("qk_prod"), i * NN + n + 1)
                nc.vector.tensor_reduce(o, src, AX.X, ALU.add).then_inc(s_("qk_sum"), 1)

            def by_neighbour(s):
                return s.rearrange("p (n x) -> p n x", n=NN)

            def scores(i):
                v.wait_ge(s_(f"qk_in{i}"), 8 * 16)
                for n in range(NN + 1):
                    if n < NN:
                        product(i, n)
                    if n:
                        channel_sum(i, n - 1)
                v.wait_ge(s_("qk_sum"), (i + 1) * NN)
                nc.vector.tensor_reduce(mx1, sc[i].rearrange("p (n x) -> p x n", n=NN), AX.X, ALU.max)\
                    .then_inc(s_("soft"), 1)
                v.wait_ge(s_("soft"), i + 1)
                nc.vector.tensor_tensor(by_neighbour(sc[i]), by_neighbour(sc[i]),
                                        mx1.unsqueeze(1).broadcast_to([P, NN, QPIX]), ALU.subtract)\
                    .then_inc(s_("sc_ready"), 1)

            def weights(i):
                v.wait_ge(s_("ex_ready"), i + 1)
                nc.vector.tensor_reduce(sm1[i], sc[i].rearrange("p (n x) -> p x n", n=NN), AX.X, ALU.add)\
                    .then_inc(s_("norm"), 1)
                v.wait_ge(s_("norm"), 3 * i + 1)
                nc.vector.reciprocal(sm1[i], sm1[i]).then_inc(s_("norm"), 1)
                v.wait_ge(s_("norm"), 3 * i + 2)
                nc.vector.tensor_tensor(by_neighbour(sc[i]), by_neighbour(sc[i]),
                                        sm1[i].unsqueeze(1).broadcast_to([P, NN, QPIX]), ALU.mult)\
                    .then_inc(s_("norm"), 1)
                v.wait_ge(s_("norm"), 3 * i + 3)

            nc.vector.memset(rt[:, 0:3 * NN * QPIX], 0.0).then_inc(s_("sc_zero"), 1)
            v.wait_ge(s_("sc_zero"), 1)
            for i in range(3):
                scores(i)
                weights(i)
            value_products(v, nc.vector, 2)
            v.wait_ge(s_("x_bias"), 2 * BLKS)
            for b in range(BLKS):
                v.wait_ge(s_("proj1_mm"), b + 1)
                xs = x_sb[:, b * TPB:(b + 1) * TPB, :].rearrange("p (h t) c -> p h t c", h=2)
                u = b % 2 * 2
                nc.vector.tensor_tensor(xs, xs, ps[:, u:u + 2, 0:2 * C].rearrange("p h (t c) -> p h t c", t=2), ALU.add)\
                    .then_inc(s_("proj1_out"), 1)
            v.wait_ge(s_("proj1_out"), BLKS)

        def attn1_tensor(pe):
            ln_tensor(pe, 2)
            with pe.Fori(0, GRP) as g:
                pe.wait_ge(s_("tp_free"), xnT_at(2, g))
                for u in range(6):
                    jj, m = u // 3, u % 3
                    pe.wait_ge(s_("qkv_staged"), g * 6 + u + 1)
                    bank = 4 + u % 2
                    nc.tensor.matmul(ps[0:KC, bank, :], wqkv1[:, m, :], xnT_v[:, jj, bass.ds(g * BT, BT)],
                                     start=True, stop=True).then_inc(s_("qkv_mm"), 1)
            for i, d in enumerate(DIL):
                if i == 2:
                    pe.wait_ge(s_("acc_ready"), 1)
                for n, (dy, dx) in enumerate(NEIGH):
                    m = i * NN + n
                    x0, w = columns(d, dx)
                    if by_pool(i, n):
                        pe.wait_ge(s_("pv_pool"), POOLS[m + 1])
                    else:
                        pe.wait_ge(s_("pv_vector"), m + 1 - POOLS[m + 1])
                    for half in range(2):
                        src = prod[2 + m % 2].rearrange("p (h y n) -> p h y n", h=2, y=2)[:, half, :, x0 * HD:(x0 + w) * HD]
                        dst = ps[:, i % 2 * 2 + half, :].rearrange("p (y n) -> p y n", y=2)[:, :, x0 * HD:(x0 + w) * HD]
                        last = nc.tensor.matmul(dst, ident, src, start=n == 0, stop=n == NN - 1, skip_group_check=True)
                    last.then_inc(s_("pv_sum"), 1)
            for b in range(BLKS):
                pe.wait_ge(s_(f"yl_in{b}"), 16)
                if b >= 2:
                    pe.wait_ge(s_("yT_ready"), b - 1)
                for k in range(2):
                    for j in range(TPB):
                        last = nc.tensor.transpose(ps[0:KC, 4 + b % 2 * 2 + k, j * P:(j + 1) * P],
                                                   yl[:, b * TPB + j, k * KC:(k + 1) * KC], ident)
                last.then_inc(s_("yl_mm"), 1)
                pe.wait_ge(s_("yT_ready"), b + 1)
                pe.wait_ge(s_("acc_ready"), 3)
                if b >= 2:
                    pe.wait_ge(s_("proj1_out"), b - 1)
                for j in range(TPB):
                    for k in range(2):
                        last = nc.tensor.matmul(ps[:, b % 2 * 2 + j // 2, j % 2 * C:(j % 2 + 1) * C],
                                                yT[b % 2][:, k, j * P:(j + 1) * P], wp[1][:, k, :],
                                                start=k == 0, stop=k == 1)
                last.then_inc(s_("proj1_mm"), 1)

        def attn1_scalar(act):
            ln_scalar(act, 2)
            for g in range(GRP):
                if g >= 2:
                    for i in range(2):
                        act.wait_ge(s_(f"qkv_out{i}{g % 2}"), 16 * QKV_DMAS // 2)
                for t in range(6):
                    act.wait_ge(s_("qkv_mm"), g * 6 + t + 1)
                    nc.scalar.activation(stage[g % 2][:, t // 3, t % 3, :], ps[0:KC, 4 + t % 2, :], ACT.Copy)\
                        .then_inc(s_("qkv_staged"), 1)
            for i in range(3):
                act.wait_ge(s_("sc_ready"), i + 1)
                nc.scalar.activation(sc[i], sc[i], ACT.Exp, scale=HD ** -0.5).then_inc(s_("ex_ready"), 1)
                if i:
                    value_sums(act, i - 1)
            value_sums(act, 2)
            for b in range(BLKS):
                act.wait_ge(s_("yl_mm"), b + 1)
                if b >= 2:
                    act.wait_ge(s_("proj1_mm"), b - 1)
                u = 4 + b % 2 * 2
                nc.scalar.activation(yT[b % 2], ps[0:KC, u:u + 2, :], ACT.Copy).then_inc(s_("yT_ready"), 1)

        def value_sums(act, i):
            act.wait_ge(s_("pv_sum"), (i + 1) * NN)
            u = i % 2 * 2
            nc.scalar.activation(acc[i].rearrange("p (h n) -> p h n", h=2), ps[:, u:u + 2, :], ACT.Copy)\
                .then_inc(s_("acc_ready"), 1)
        @block.sync
        def _(sp):
            for b in range(BLKS):
                sp.dma_start(x_sb[:, b * TPB:(b + 1) * TPB, :],
                             a["x"].rearrange("(t p) c -> p t c", p=P)[:, b * TPB:(b + 1) * TPB, :])\
                    .then_inc(s_("x_in"), 16)
            sp.dma_start(cst[:], a["cst"]).then_inc(s_("cst_in"), 16)
            sp.dma_start(wqk0[:], a["wqk0"]).then_inc(s_("wqk_in"), 16)
            sp.dma_start(bqk0[:], a["bqk0"]).then_inc(s_("wqk_in"), 16)
            sp.dma_start(cq, a["cq"]).then_inc(s_("cqk_in"), 16)
            sp.dma_start(ck, a["ck"]).then_inc(s_("cqk_in"), 16)
            sp.dma_start(padf, a["cpad"].unsqueeze(1).broadcast_to([P, NH, PADS])).then_inc(s_("padf_in"), 16)
            for i, name in enumerate(("relh", "relw")):
                sp.dma_start(relt[i], a[name]).then_inc(s_("rel_in"), 16)
            small = [(wv0, "wv0"), (bv0, "bv0"), (wqkv1, "wqkv1")]
            for l in range(2):
                small += [(wp[l], f"wp{l}"), (bp[l], f"bp{l}"), (wg[l], f"wg{l}"), (bg[l], f"bg{l}")]
            for t, name in small:
                sp.dma_start(t[:], a[name]).then_inc(s_("small_in"), 16)
            sp.wait_ge(s_("kps_ready"), 2)
            for g in range(2):
                sp.dma_start(kpd[g * HG:(g + 1) * HG].rearrange("h c n -> (h c) n"), kps[:, g, :])\
                    .then_inc(s_("kpd_out"), 16)
            sp.wait_ge(s_("kpd_out"), 32)
            sp.wait_ge(s_("padf_in"), 16)
            for r in (R_HI, R_DUP, R_LO):
                sp.dma_start(padf[r:r + HD], kpd.rearrange("h c n -> c h n")).then_inc(s_("padf_in"), 16)
            for k in range(8):
                if k < 2:
                    sp.wait_ge(s_("k_free"), 2 + 2 * BLKS)
                else:
                    sp.wait_ge(s_("staged"), k - 1)
                g, src = k % 2, pt[k % 3]
                hs = slice(g * HG, (g + 1) * HG)
                if k < 2:
                    dst, rows = kd[hs], KC
                elif k < 4:
                    dst, rows = qd[hs, 0:HD], KC
                else:
                    r = HD + WS * (k // 2 - 2)
                    dst, rows = qd[hs, r:r + WS], HG * WS
                sp.dma_start(dst, src[0:rows]).then_inc(s_(f"stored{k}"), 16)
            for k in range(8):
                sp.wait_ge(s_(f"stored{k}"), 16)
            sp.wait_ge(s_("small_in"), 16 * 11)
            attn0_sync(sp)
            moe_sync(sp, 0)
            attn1_sync(sp)
            moe_sync(sp, 1)
            for b in range(BLKS):
                sp.wait_ge(s_("combined"), BLKS + b + 1)
                sp.dma_start(out[b * BT:(b + 1) * BT].rearrange("(t p) c -> p t c", p=P),
                             x_sb[:, b * TPB:(b + 1) * TPB]).then_inc(s_("out"), 16)
            sp.wait_ge(s_("out"), 16 * BLKS)

        @block.vector
        def _(v):
            v.wait_ge(s_("cst_in"), 16)
            nc.vector.tensor_copy(cstb[:, 0:3 * P], cst[:, P:4 * P]).then_inc(s_("bf_cst"), 1)
            at = CST_AT["ida"]
            nc.vector.tensor_copy(cstb[:, 3 * P:], cst[:, at:at + 64 + SLOTS]).then_inc(s_("bf_cst"), 1)
            nc.vector.memset(kpz, 0.0).then_inc(s_("kpz"), 1)
            v.wait_ge(s_("kpz"), 1)
            v.wait_ge(s_("wqk_in"), 32)
            for g in range(2):
                nc.vector.tensor_scalar(kps[:, g, :], kpz, bqk0[:, 2 + g:3 + g], HD ** -0.5, ALU.add, ALU.mult)\
                    .then_inc(s_("kps_ready"), 1)
            v.wait_ge(s_("x_in"), 16 * BLKS)
            ln_vector(v, 0)
            with v.Fori(0, BLKS) as b:
                for g in range(2):
                    v.wait_ge(s_("k_mm"), b * 2 + g + 1)
                    src = ps[0:KC, 6 + g, :].rearrange("p (i y x) -> p i y x", i=2, y=SIDE)
                    blk = pt[g][0:KC, bass.ds(b * BT, BT)]
                    n0 = 2 * WA
                    outs = (blk[:, 0:n0].rearrange("p (i y x) -> p i y x", i=2, x=WS),
                            blk[:, n0:BT].rearrange("p (i n) -> p i n", i=2)[:, :, 0:NBD]
                            .rearrange("p i (y x) -> p i y x", x=SIDE - WS),
                            blk[:, n0:BT].rearrange("p (i n) -> p i n", i=2)[:, :, NBD:NB1]
                            .rearrange("p i (y x) -> p i y x", x=WS))
                    ins = (src[:, :, 0:WS, 0:WS], src[:, :, :, WS:SIDE], src[:, :, WS:SIDE, 0:WS])
                    for o, i in zip(outs, ins):
                        last = nc.vector.tensor_scalar(o, i, bqk0[:, 2 + g:3 + g], HD ** -0.5, ALU.add, ALU.mult)
                    last.then_inc(s_("k_free"), 1)
            v.wait_ge(s_("pk_hi"), 1)
            nc.vector.tensor_tensor(pk[R_DUP:R_DUP + HD], padf[R_DUP:R_DUP + HD],
                                    pk[R_DUP:R_DUP + HD].bitcast(F32), ALU.subtract).then_inc(s_("pk_ready"), 1)
            for k in range(2, 8):
                if k < 4:
                    v.wait_ge(s_("q_ready"), 2 + 2 * BLKS)
                    src, rows = qT[:, k - 2, :], KC
                else:
                    v.wait_ge(s_("rel_out"), 4 * (k - 3))
                    src, rows = rn[k % 2], HG * WS
                if k >= 3:
                    v.wait_ge(s_(f"stored{k - 3}"), 16)
                permute(pt[k % 3], src, rows).then_inc(s_("staged"), 1)
            attn0_vector(v)
            moe_vector(v, 0)
            attn1_vector(v)
            moe_vector(v, 1)

        @block.tensor
        def _(pe):
            pe.wait_ge(s_("cst_in"), 16)
            ln_tensor(pe, 0)
            pe.wait_ge(s_("wqk_in"), 32)
            with pe.Fori(0, BLKS) as b:
                pe.wait_ge(s_("tp_free"), b + 3)
                for m in range(4):
                    pe.wait_ge(s_("q_ready" if m < 2 else "k_free"), b * 2 + m % 2 + 1)
                    for k in range(2):
                        last = nc.tensor.matmul(ps[0:KC, 4 + m, :], wqk0[:, k, m, :],
                                                xnT_v[:, k, bass.ds(b * BT, BT)], start=k == 0, stop=k == 1)
                    last.then_inc(s_("q_mm" if m < 2 else "k_mm"), 1)
            pe.wait_ge(s_("rel_in"), 32)
            pe.wait_ge(s_("q_ready"), 2 + 2 * BLKS)
            for n in range(16):
                w, g, quarter = n // 8, n // 4 % 2, n % 4
                if n >= 4:
                    pe.wait_ge(s_("rel_out"), n - 3)
                img = qT[:, g, :].rearrange("p (i y x) -> p i y x", i=IMGS, y=SIDE)
                for u in range(4):
                    at = 4 * quarter + u
                    rhs = img[:, :, at, :] if w == 0 else img[:, :, :, at]
                    last = nc.tensor.matmul(ps[0:HG * WS, n % 4, u * P:(u + 1) * P], relt[w][:, at % WS, :], rhs,
                                            start=True, stop=True)
                last.then_inc(s_("rel_mm"), 1)
            attn0_tensor(pe)
            moe_tensor(pe, 0)
            attn1_tensor(pe)
            moe_tensor(pe, 1)

        @block.scalar
        def _(act):
            act.wait_ge(s_("cqk_in"), 32)
            for dst, src in ((q0, cq), (k0, ck)):
                nc.scalar.activation(dst[KC:R_MAX + 1].rearrange("p c h n -> p (c h) n"),
                                     src[KC:R_MAX + 1].unsqueeze(1).broadcast_to([R_MAX + 1 - KC, NH, BT]),
                                     ACT.Copy).then_inc(s_("rows_set"), 1)
            ln_scalar(act, 0)
            with act.Fori(0, BLKS) as b:
                for g in range(2):
                    act.wait_ge(s_("q_mm"), b * 2 + g + 1)
                    nc.scalar.activation(qT[:, g, bass.ds(b * BT, BT)], ps[0:KC, 4 + g, :], ACT.Identity,
                                         bias=bqk0[:, g:g + 1]).then_inc(s_("q_ready"), 1)
            act.wait_ge(s_("padf_in"), 64)
            act.wait_ge(s_("q_ready"), 2 + 2 * BLKS)
            nc.scalar.activation(pk[0:R_MAX + 1], padf[0:R_MAX + 1], ACT.Copy).then_inc(s_("pk_hi"), 1)
            for n in range(16):
                w, g, quarter = n // 8, n // 4 % 2, n % 4
                k = n // 4
                if k >= 2 and quarter == 0:
                    act.wait_ge(s_("staged"), k + 1)
                act.wait_ge(s_("rel_mm"), n + 1)
                src = ps[0:HG * WS, n % 4, :]
                if w == 0:
                    d = rn[k % 2][0:HG * WS].rearrange("p (i y x) -> p y i x", i=IMGS, y=SIDE)
                    s = src.rearrange("p (y i x) -> p y i x", y=4, i=IMGS)
                else:
                    d = rn[k % 2][0:HG * WS].rearrange("p (r x) -> p x r", x=SIDE)
                    s = src.rearrange("p (x r) -> p x r", x=4)
                nc.scalar.activation(d[:, 4 * quarter:4 * quarter + 4], s, ACT.Copy).then_inc(s_("rel_out"), 1)
            attn0_scalar(act)
            moe_scalar(act, 0)
            attn1_scalar(act)
            moe_scalar(act, 1)

        @block.gpsimd
        def _(pool):
            for k, (name, n) in enumerate((("xn_free", 2), ("tp_free", 2), ("q_ready", 2),
                                           ("k_free", 2), ("pv_done", 1), ("qkv_staged", 2),
                                           ("misc_full", 1), ("misc_free", 1))):
                nc.gpsimd.memset(credit[0:1, k:k + 1], 0.0).then_inc(s_(name), n)
            attn0_pool(pool)
            moe_pool(pool, 0)
            attn1_pool(pool)
            moe_pool(pool, 1)


INPUTS = ["x", "cst", "wqk0", "bqk0", "cq", "ck", "cpad", "relh", "relw", "wv0", "bv0", "wqkv1", "wp0", "bp0", "wg0", "bg0",
          "wp1", "bp1", "wg1", "bg1", "cq1", "ck1", "w1_0", "w2_0", "b2_0", "w1_1", "w2_1", "b2_1"]


def layout(i):
    import numpy as np

    f = np.float32
    o = {"x": i["x"].reshape(T, C)}

    def halves(w):
        return np.ascontiguousarray(w.reshape(2, KC, -1).transpose(1, 0, 2))

    def rows(b):
        return np.ascontiguousarray(np.broadcast_to(b.reshape(1, -1), (P, b.size)))

    w, b = i["L0_conv_qkv_w"], i["L0_conv_qkv_b"]
    o["wqk0"] = halves(w[:2 * C].T).reshape(KC, 2, 4, KC)
    o["bqk0"] = np.ascontiguousarray(b[:2 * C].reshape(4, KC).T)
    o["wv0"], o["bv0"] = halves(w[2 * C:].T), rows(b[2 * C:])
    for name, r in (("relh", i["L0_conv_rel_pos_h"]), ("relw", i["L0_conv_rel_pos_w"])):
        t = np.zeros((HG, HD, WS, HG, WS), f)
        for h in range(HG):
            for q in range(WS):
                for k in range(WS):
                    t[h, :, q, h, k] = r[q - k + WS - 1]
        o[name] = t.reshape(KC, WS, HG * WS)
    o["wp0"], o["bp0"] = halves(i["L0_conv_proj_w"].T), rows(i["L0_conv_proj_b"])
    o["wp1"], o["bp1"] = halves(i["L1_conv_proj_w"].T), rows(i["L1_conv_proj_b"])
    wd = np.zeros((2, GCH, 2, 3 * GCH), f)
    for j in range(2):
        wd[j, :, j] = i["L1_conv_qkv_w"].T
    o["wqkv1"] = wd.reshape(KC, 3, KC)
    o["wg0"], o["bg0"] = halves(i["L0_ffn_Wg"]), rows(i["L0_ffn_bg"])
    o["wg1"], o["bg1"] = halves(i["L1_ffn_gate_w"].T), np.zeros((P, E), f)
    for l, n in enumerate((("L0_ffn_W1", "L0_ffn_b1", "L0_ffn_W2", "L0_ffn_b2"),
                           ("L1_ffn_w1", "L1_ffn_b1", "L1_ffn_w2", "L1_ffn_b2"))):
        w1 = np.zeros((E, KC + 1, 2, F), f)
        w1[:, :KC] = i[n[0]].reshape(E, 2, KC, F).transpose(0, 2, 1, 3)
        w1[:, KC, 0] = i[n[1]]
        o[f"w1_{l}"] = w1
        o[f"w2_{l}"] = np.ascontiguousarray(i[n[2]].reshape(E, FT, P, C).transpose(0, 2, 1, 3))
        o[f"b2_{l}"] = rows(i[n[3]])

    y, x = np.divmod(np.arange(PIX), SIDE)
    order = [(y < WS) & (x < WS), x >= WS, (y >= WS) & (x < WS)]
    own = np.concatenate([np.flatnonzero(m) for m in order])
    tok = np.concatenate([own[:WA], own[:WA], own[WA:], own[WA:]])
    img = np.concatenate([np.zeros(WA), np.ones(WA), np.zeros(NB1), np.ones(NB1)]).astype(int)
    win = (y // WS * 2 + x // WS)[tok]
    hot = np.zeros((2 * WS, BT), f)
    hot[(y % WS)[tok], np.arange(BT)] = 1
    hot[WS + (x % WS)[tok], np.arange(BT)] = 1

    def key_rows(k, hot):
        k[R_REL1:R_REL1 + HD], k[R_REL2:R_REL2 + 2 * WS - HD] = hot[:HD], hot[HD:]
        k[R_RELLO:R_RELLO + 2 * WS] = hot
        k[R_MAX] = 1

    cq, ck, cp = np.zeros((P, BT), f), np.zeros((P, BT), f), np.zeros((P, PADS), f)
    key_rows(ck, hot)
    py, px = np.divmod(np.arange(WA), WS)
    hot = np.zeros((2 * WS, PADS), f)
    hot[py, np.arange(WA)] = 1
    hot[WS + px, np.arange(WA)] = 1
    key_rows(cp, hot)
    edge = SIDE - WS
    for n in range(2):
        for m in range(1, 4):
            r = R_WIN + 3 * n + m - 1
            mine = (img == n) & (win == m)
            cq[r, mine] = NEG
            ck[r, 2 * WA:] = ~mine[2 * WA:]
            cp[r, :WA] = ((px < edge) | (m == 2)) & ((py < edge) | (m == 1))
            cp[r, WA:] = 1
    o["cq"], o["ck"], o["cpad"] = cq, ck, cp

    cq1, ck1 = np.zeros((P, len(DIL), PIX), f), np.zeros((P, PIX), f)
    npad = np.zeros((P, len(DIL), 2), f)
    for n, d in enumerate(DIL):
        for k in range(SIDE):
            cq1[R_REL1 + k, n, ~np.isin(k - y, (-d, 0, d))] = NEG
            cq1[R_REL2 + k, n, ~np.isin(k - x, (-d, 0, d))] = NEG
        inside = lambda v: sum((0 <= v + s) & (v + s < SIDE) for s in (-d, 0, d))
        npad[:, n] = (9 - inside(y) * inside(x)).reshape(2, P).T
    ck1[R_REL1 + y, np.arange(PIX)] = 1
    ck1[R_REL2 + x, np.arange(PIX)] = 1
    ck1[L1_ROWS] = 1
    o["cq1"], o["ck1"] = cq1, ck1

    p, e, s = np.arange(P), np.arange(E), np.arange(SLOTS)
    token = np.arange(TILES)[None, :] * P + p[:, None]
    ids = np.stack([2 * token + k + 1 for k in range(2)], 1).reshape(P, -1)
    sel = np.zeros((P, KC), f)
    sel[KC + np.arange(KC) // HD, np.arange(KC)] = 1
    o["cst"] = np.concatenate([
        np.eye(P), p[:, None] < p[None, :], np.tile(p, (P, 1)), np.ones((P, P)), np.tile(E - e, (P, 1)),
        np.tile((e[None, :] < e[:, None]).reshape(-1), (P, 1)), np.tile(np.arange(16) * P, (P, 1)),
        ids // 64, ids % 64, np.tile(s, (P, 1)), npad.reshape(P, -1),
        np.where(npad > 0, 0, NEG).reshape(P, -1), sel], 1).astype(f)
    return {k: np.ascontiguousarray(o[k]) for k in INPUTS}


def kernel(**inputs):
    import numpy as np
    import concourse.bacc as bacc
    from concourse.bass_utils import run_bass_kernel_spmd

    arrays = layout({k: np.asarray(v) for k, v in inputs.items()})
    nc = bacc.Bacc("TRN2", target_bir_lowering=False, num_devices=1)
    aps = {k: nc.dram_tensor(f"in_{k}", v.shape, mybir.dt.from_np(v.dtype), kind="ExternalInput").ap()
           for k, v in arrays.items()}
    out = nc.dram_tensor("out_x", [T, C], F32, kind="ExternalOutput").ap()
    build(nc, aps, out)
    result = run_bass_kernel_spmd(nc, [{f"in_{k}": v for k, v in arrays.items()}], core_ids=[0])
    return result.results[0]["out_x"].reshape(IMGS, SIDE, SIDE, C)
```

```python
from contextlib import ExitStack

import concourse.bass as bass
from concourse import mybir

F32 = mybir.dt.float32
F32R = mybir.dt.float32r
BF16 = mybir.dt.bfloat16
I32 = mybir.dt.int32
ALU = mybir.AluOpType
ACT = mybir.ActivationFunctionType
AX = mybir.AxisListType

P = 128
IMGS, SIDE, C = 8, 16, 192
PIX = SIDE * SIDE
T = IMGS * PIX
TILES = T // P
KC = 96
BLKS = 4
BT = T // BLKS
TPB = BT // P
NEG = -float(2 ** 30)

WS, NH, HD = 14, 12, 16
WA = WS * WS
WAH = WA // 2
NBD = SIDE * (SIDE - WS)
NBC = (SIDE - WS) * WS
NB1 = NBD + NBC
NB = 2 * NB1
PADS = 240
HG = 6
HC = 3
CPB = NH // HC
QROWS = HD + 2 * WS
VW = HG * HD + HG
VS = HG * (HD + VW)
R_HI, R_REL1, R_DUP, R_REL2, R_LO, R_RELLO = 0, 16, 32, 48, 64, 80
R_ROUND = 108
R_WIN = 108
K_MAX = 114
R_MAX = 114

DIL = (1, 2, 3)
GRP, GCH = 4, C // 4
SPU = 8

E, F, FT = 8, 768, 768 // P
SLOTS = 42
MT = (2 * T - E) // P + E
W1C, W2C = 2 * F, FT * C
LN_EPS = (1e-6, 1e-5, 1e-6, 1e-5)




def build(nc, a, out):
    ctx = ExitStack()
    with ctx:
        def sb(name, shape, dt=F32):
            return ctx.enter_context(nc.sbuf_tensor(name, shape, dt))

        def sem(name):
            return ctx.enter_context(nc.semaphore(name))

        def dram(name, shape):
            return nc.dram_tensor(name, shape, F32, kind="Internal").ap()

        qd = dram("qd", [NH, QROWS, T])
        kd = dram("kd", [NH, HD, T])
        kpd = dram("kpd", [NH, HD, PADS])
        xnd = [dram(f"xnd{l}", [T, C]) for l in range(2)]
        yd = [dram(f"yd{l}", [2 * T, C]) for l in range(2)]
        qkvd = dram("qkvd", [SPU * 3 * len(DIL), GRP, HD, PIX])
        y1d = dram("y1d", [GRP * len(DIL) * SPU, PIX, HD])

        x_sb = sb("x_sb", [P, TILES, C])
        xnT = sb("xnT", [P, 4096])
        xnT_v = xnT[0:KC, :].rearrange("p (k t) -> p k t", k=2)
        xn = sb("xn", [P, 2, TPB, C])
        cst = sb("cst", [P, a["cst"].shape[1]])
        wv0 = sb("wv0", [KC, 2, C])
        wp = [sb(f"wp{l}", [KC, 2, C]) for l in range(2)]
        bp = [sb(f"bp{l}", [P, C]) for l in range(2)]
        bv0 = sb("bv0", [P, C])
        wqkv1 = sb("wqkv1", [KC, 3, KC])
        wg = [sb(f"wg{l}", [KC, 2, E]) for l in range(2)]
        bg = [sb(f"bg{l}", [P, E]) for l in range(2)]
        bqk0 = sb("bqk0", [KC, 4])
        stats = sb("stats", [P, 2, TPB, 6])
        mv = sb("mv", [P, 2, TPB, 2])
        rstd = sb("rstd", [P, 2, TPB])
        veps = sb("veps", [P, 2, TPB])
        newton = sb("newton", [P, 2, TPB])
        credit = sb("credit", [1, 16])
        arena = sb("arena", [P, E * (W1C + W2C)])
        qq = sb("qq", [P, 6144], F32R)
        kk = sb("kk", [P, 6144], F32R)
        pk = sb("pk", [P, NH, PADS], F32R)
        nm = sb("nm", [HC, 2, BT], F32R)
        gw = sb("gw", [P, 2, TILES])
        gidx = sb("gidx", [P, SLOTS], I32)
        sidx = sb("sidx", [P, SLOTS], I32)
        gcur = sb("gcur", [P, 3], I32)
        scur = sb("scur", [P, 3], I32)
        te = sb("te", [1, SLOTS], I32)
        rt = sb("rt", [P, 2816])
        cstb = sb("cstb", [P, 3 * P + 2 * 32 + SLOTS], BF16)
        smallb = sb("smallb", [P, 64], BF16)
        hotb = sb("hotb", [P, 2 * TILES * E], BF16)
        hotb_v = hotb[:, :].rearrange("p (c e) -> p c e", e=E)
        ROUTE_STEPS = [0]
        ps = ctx.enter_context(nc.psum_tensor("ps", [P, 8, 512], F32))

        at = 0
        CST, CST_AT = {}, {}
        for name, n in (("ident", 128), ("tri", 128), ("iot", 128), ("ones", 128), ("rev", E), ("lt", E * E),
                        ("ida", 32), ("idb", 32), ("iots", SLOTS), ("sel", KC)):
            CST[name], CST_AT[name] = cst[:, at:at + n], at
            at += n
        ident = CST["ident"]
        trib, iotb, onesb = (cstb[:, i * P:(i + 1) * P] for i in range(3))
        idab, idbb, iotsb = cstb[:, 384:416], cstb[:, 416:448], cstb[:, 448:448 + SLOTS]

        def ar(word, shape, parts=P):
            n = 1
            for s in shape:
                n *= s
            v = arena[0:parts, word:word + n]
            names = "abcd"[:len(shape)]
            if len(shape) > 1:
                v = v.rearrange(f"p ({' '.join(names)}) -> p {' '.join(names)}",
                                **{k: s for k, s in zip(names, shape)})
            return v

        def xt_(word, shape, parts=P):
            n = 1
            for s in shape:
                n *= s
            v = xnT[0:parts, word:word + n]
            names = "abcd"[:len(shape)]
            if len(shape) > 1:
                v = v.rearrange(f"p ({' '.join(names)}) -> p {' '.join(names)}",
                                **{k: s for k, s in zip(names, shape)})
            return v

        padf = ar(0, [NH, PADS])
        qT = ar(2880, [2, T], KC)
        pt = [ar(6976 + 2048 * i, [T]) for i in range(3)]
        rn = [ar(13120 + 2048 * i, [T]) for i in range(2)]
        cq = ar(20336, [BT])
        ck = ar(20336 + BT, [BT])
        kpz = ar(13120 + 1024, [PADS], KC)
        kps = ar(13120 + 1024 + PADS, [2, PADS], KC)
        relt = [ar(17216 + 1176 * i, [WS, HG * WS], KC) for i in range(2)]
        wqk0 = ar(19568, [2, 4, KC], KC)
        fq = [ar(1536 * i, [HC, BT]) for i in range(2)]
        fk = [ar(3072 + 1536 * i, [HC, BT]) for i in range(2)]
        v0 = ar(6144, [2, 5, VS])
        pa = [ar(13224 + 1144 * i, [2, 2 * WA]) for i in range(2)]
        pb = [ar(13224 + 1144 * i + 784, [3, NB]) for i in range(2)]
        osb = ar(15512, [BT])
        ot = ar(16536, [2, BT], KC)
        vpad = ar(17560, [2, VS])
        xp = ar(18976, [2, BT], KC)
        mxa = ar(20000, [2, 4, HC])
        mxb = ar(20024, [2, HC])

        w1s = ar(0, [E, 2, F], KC + 1)
        w2s = ar(E * W1C, [E, FT, C])
        xn2 = w2s[:, E - 2:E].rearrange("p e f c -> p (e f c)")[:, 0:2 * TPB * C]\
            .rearrange("p (u t c) -> p u t c", u=2, t=TPB)
        lg = rt[0:E, 976:976 + 2 * BT].rearrange("p (u n) -> p u n", u=2)
        wcur = [[xt_(F * r, [F], KC + 1), rt[0:KC + 1, F * r:F * (r + 1)]] for r in range(3)]
        hidT = xt_(3 * F, [FT, P])
        xgT = xt_(4 * F, [2, P], KC + 1)
        xg = [xt_(4 * F + 2 * P + C * r, [C]) for r in range(3)]
        ys = [xt_(4 * F + 2 * P + C * 3, [C])] + [rt[:, 3 * F + C * r:3 * F + C * (r + 1)] for r in range(2)]
        b2s = xn[:, :, :, :].rearrange("p u t c -> p (u t) c")
        yt = ar(0, [TILES, 2, C])

        q0 = qq[:, :].rearrange("p (c h n) -> p c h n", c=CPB, h=HC)
        k0 = kk[:, :].rearrange("p (c h n) -> p c h n", c=CPB, h=HC)

        S = {}

        def s_(name):
            if name not in S:
                S[name] = sem(name)
            return S[name]

        def blocks_of(v):
            return v.rearrange("p (b i y x) -> p b i y x", b=BLKS, i=2, y=SIDE)

        block = ctx.enter_context(nc.Block())

        def normed(n, b):
            return xn[:, b % 2] if b < 2 or n % 2 == 0 else xn2[:, b % 2]

        def ln_statistics(v, n, turn):
            if n == 0:
                for u in range(2):
                    v.wait_ge(s_(f"x_in{turn * 2 + u}"), 16)
            for u in range(2):
                for j in range(TPB):
                    t = (turn * 2 + u) * TPB + j
                    last = nc.vector.bn_stats(stats[:, u, j, :], x_sb[:, t, :])
            last.then_inc(s_("ln_stats"), 1)
            v.wait_ge(s_("ln_stats"), n * 2 + turn + 1)
            for u in range(2):
                for j in range(TPB):
                    last = nc.vector.bn_aggr(mv[:, u, j, :], stats[:, u, j, :])
            last.then_inc(s_("ln_mv"), 1)
            v.wait_ge(s_("ln_mv"), n * 2 + turn + 1)
            nc.vector.tensor_scalar(veps[:], mv[:, :, :, 1], LN_EPS[n], None, ALU.add).then_inc(s_("ln_eps"), 1)

        def ln_normalise(v, n, turn):
            v.wait_ge(s_("ln_sqrt"), n * 2 + turn + 1)
            nc.vector.reciprocal(rstd[:], rstd[:]).then_inc(s_("ln_step"), 1)
            done = (n * 2 + turn) * 4
            v.wait_ge(s_("ln_step"), done + 1)
            nc.vector.tensor_tensor(newton[:], rstd[:], rstd[:], ALU.mult).then_inc(s_("ln_step"), 1)
            v.wait_ge(s_("ln_step"), done + 2)
            nc.vector.tensor_tensor(newton[:], newton[:], veps[:], ALU.mult).then_inc(s_("ln_step"), 1)
            v.wait_ge(s_("ln_step"), done + 3)
            nc.vector.tensor_scalar(newton[:], newton[:], -0.5, 1.5, ALU.mult, ALU.add).then_inc(s_("ln_step"), 1)
            v.wait_ge(s_("ln_step"), done + 4)
            nc.vector.tensor_tensor(rstd[:], rstd[:], newton[:], ALU.mult).then_inc(s_("ln_rstd"), 1)
            v.wait_ge(s_("ln_rstd"), n * 2 + turn + 1)
            for u in range(2):
                b = turn * 2 + u
                v.wait_ge(s_("xn_free"), n * BLKS + b + 1)
                for j in range(TPB):
                    last = nc.vector.tensor_scalar(normed(n, b)[:, j, :], x_sb[:, b * TPB + j, :], mv[:, u, j, 0:1],
                                                   rstd[:, u, j:j + 1], ALU.subtract, ALU.mult)
                last.then_inc(s_("xn_ready"), 1)

        def ln_vector(v, n, turns=(0, 1)):
            for turn in turns:
                ln_statistics(v, n, turn)
                ln_normalise(v, n, turn)

        def ln_transpose(pe, n, b, u):
            source = xn[:, u] if n % 2 == 0 else normed(n, b)
            pe.wait_ge(s_("xn_ready"), n * BLKS + b + 1)
            pe.wait_ge(s_("tp_free"), n * BLKS + b + 1)
            for k in range(2):
                for j in range(TPB):
                    last = nc.tensor.transpose(ps[0:KC, 2 * u + k, j * P:(j + 1) * P],
                                               source[:, j, k * KC:(k + 1) * KC], ident)
            last.then_inc(s_("xn_free"), 1)

        def ln_tensor(pe, n):
            with pe.Fori(0, 2) as turn:
                for u in range(2):
                    ln_transpose(pe, n, turn * 2 + u, u)

        def ln_root(act, n, turn):
            act.wait_ge(s_("ln_eps"), n * 2 + turn + 1)
            nc.scalar.activation(rstd[:], veps[:], ACT.Sqrt).then_inc(s_("ln_sqrt"), 1)

        def ln_copy(act, n, b):
            act.wait_ge(s_("xn_free"), n * BLKS + b + 1 + 2)
            u = b % 2 * 2
            nc.scalar.activation(xnT_v[:, :, b * BT:(b + 1) * BT], ps[0:KC, u:u + 2, :], ACT.Copy)\
                .then_inc(s_("tp_free"), 1)

        def ln_scalar(act, n):
            for b in range(BLKS):
                if b % 2 == 0:
                    ln_root(act, n, b // 2)
                ln_copy(act, n, b)

        def xnT_at(n, b):
            return n * BLKS + b + 3

        def perm_out(dst, i):
            n0 = 2 * WA + i * NB1
            return (dst[:, :, i * WA:(i + 1) * WA].rearrange("p b (y x) -> p b y x", x=WS),
                    dst[:, :, n0:n0 + NBD].rearrange("p b (y x) -> p b y x", x=SIDE - WS),
                    dst[:, :, n0 + NBD:n0 + NB1].rearrange("p b (y x) -> p b y x", x=WS))

        def perm_in(src, i):
            return (src[:, :, i, 0:WS, 0:WS], src[:, :, i, :, WS:SIDE], src[:, :, i, WS:SIDE, 0:WS])

        def permute(dst, src, rows):
            d = dst[0:rows].rearrange("p (b n) -> p b n", b=BLKS)
            s = blocks_of(src[0:rows])
            for i in range(2):
                for o, n in zip(perm_out(d, i), perm_in(s, i)):
                    last = nc.vector.tensor_copy(o, n)
            return last


        ST_A, ST_B, SM_A, SM_B, PV, MISC = 0, 2, 3, 5, 6, 7
        TR0_, R1_, TR1_, PA_, PB_, V1_, TR2_, R0_, TR3_, V0_ = range(10)
        AHEAD = 3

        def tr_use(blk, cc, first):
            return blk * 10 + ((AHEAD, AHEAD + 1, TR2_, TR3_) if first else (TR0_, TR1_, TR2_, TR3_))[cc]

        def peeled(eng, body):
            body(0, True, False)
            with eng.Fori(1, BLKS - 1) as blk:
                body(blk, False, False)
            body(BLKS - 1, False, True)

        def attn0_sync(sp):
            def load_q(blk, cc):
                f, hs, cols = fq[cc % 2], slice(cc * HC, (cc + 1) * HC), bass.ds(blk * BT, BT)
                for r, lo, hi in ((0, 0, 32), (R_DUP, 0, HD), (R_REL2, 2 * HD, QROWS), (R_LO, 0, QROWS)):
                    sp.dma_start(f[r:r + hi - lo], qd[hs, lo:hi, cols].rearrange("h c n -> c h n"))\
                        .then_inc(s_(f"fq_in{cc % 2}"), 16)

            def load_k(blk, cc):
                g, hs, cols = fk[cc % 2], slice(cc * HC, (cc + 1) * HC), bass.ds(blk * BT, BT)
                for r in (R_HI, R_DUP, R_LO):
                    sp.dma_start(g[r:r + HD], kd[hs, :, cols].rearrange("h c n -> c h n"))\
                        .then_inc(s_(f"fk_in{cc % 2}"), 16)

            def minus_max(n, cc):
                sp.wait_ge(s_("misc_free"), n + 1)
                sp.dma_start(q0[R_MAX:R_MAX + 1, cc].bitcast(F32), nm[0:HC, cc % 2, :].bitcast(F32))\
                    .then_inc(s_(f"nm_in{cc % 2}"), 16)

            sp.wait_ge(s_("pk_ready"), 1)
            sp.wait_ge(s_("fq_zero"), 1)
            sp.wait_ge(s_("fk_rows"), 2)
            for k in range(2):
                sp.wait_ge(s_(f"stored{k}"), 16)
                load_k(0, k)
            for c in range(CPB):
                if c % 2 == 0:
                    for k in range(2 + c // 2, 8, 2):
                        sp.wait_ge(s_(f"stored{k}"), 16)
                if c >= 2:
                    sp.wait_ge(s_("q_lo"), c - 1)
                    sp.wait_ge(s_("k_lo"), c - 1)
                load_q(0, c)
                if c >= 2:
                    load_k(0, c)
            minus_max(2, 0)

            def body(blk, first, last):
                for cc in range(CPB):
                    chunk = blk * CPB + cc
                    if not (last and cc == 3):
                        minus_max(tr_use(blk, cc, first), (cc + 1) % CPB)
                    if not last:
                        sp.wait_ge(s_("q_lo"), chunk + 3)
                        sp.wait_ge(s_("k_lo"), chunk + 3)
                        load_q(blk + 1, cc)
                        load_k(blk + 1, cc)

            peeled(sp, body)

        def attn0_pool(pool):
            def window_order(blk, lows):
                pool.wait_ge(s_("k_lo"), lows)
                s = xnT_v[:, :, bass.ds(blk * BT, BT)].rearrange("p k (i y x) -> p k i y x", i=2, y=SIDE)
                for i in range(2):
                    for o, n in zip(perm_out(xp, i), perm_in(s, i)):
                        last = nc.gpsimd.tensor_copy(o, n)
                last.then_inc(s_("xp_ready"), 1)

            def k_low(chunk, cc, orders):
                pool.wait_ge(s_("xp_ready"), orders)
                pool.wait_ge(s_("k_lo"), chunk)
                pool.wait_ge(s_("k_rnd"), chunk + 1)
                dst = k0[R_DUP:R_DUP + HD, cc]
                nc.gpsimd.tensor_tensor(dst, fk[cc % 2][R_DUP:R_DUP + HD], dst.bitcast(F32), ALU.subtract)\
                    .then_inc(s_("k_lo"), 1)

            pool.wait_ge(s_("xn_ready"), BLKS)
            pool.wait_ge(s_("small_in"), 16 * 11)
            for b in range(BLKS):
                xs = x_sb[:, b * TPB:(b + 1) * TPB, :]
                nc.gpsimd.tensor_tensor(xs, xs, bp[0][:].unsqueeze(1).broadcast_to([P, TPB, C]), ALU.add)\
                    .then_inc(s_("x_bias"), 1)
            pool.wait_ge(s_("x_bias"), BLKS)
            pool.wait_ge(s_("rel_out"), 16)
            pool.wait_ge(s_("tp_free"), xnT_at(0, BLKS - 1))
            window_order(0, 0)
            for k in range(5, 8):
                pool.wait_ge(s_(f"stored{k}"), 16)
            pool.wait_ge(s_("xp_ready"), 1)
            nc.gpsimd.memset(v0, 0.0).then_inc(s_("v0_zero"), 1)
            pool.wait_ge(s_("v0_zero"), 1)
            for c in range(3):
                k_low(c, c, 1)

            def body(blk, first, last):
                for cc in range(CPB):
                    if not (last and cc >= 1):
                        k_low(blk * CPB + cc + 3, (cc + 3) % CPB, blk + 1 + (cc > 1))
                    if cc == 1 and not last:
                        pool.wait_ge(s_("misc_full"), blk * 10 + V1_ + 1)
                        window_order(blk + 1, blk * CPB + 5)

            peeled(pool, body)

        def attn0_vector(v):
            def maxima(chunk, cc, j):
                v.wait_ge(s_("sm_done"), chunk * HC + j + 1)
                nc.vector.tensor_reduce(mxa[0:WAH, cc % 2, :, j],
                                        ps[0:WAH, SM_A:SM_A + 2, 0:2 * WA].rearrange("p i (q n) -> p i q n", q=2),
                                        AX.X, ALU.max)
                nc.vector.tensor_reduce(mxb[0:NB, cc % 2, j:j + 1], ps[0:NB, SM_B, 0:NB + PADS], AX.X, ALU.max)\
                    .then_inc(s_("max_done"), 1)

            def minus(n, chunk, cc):
                v.wait_ge(s_("misc_full"), n + 1)
                nc.vector.tensor_scalar(nm[0:HC, cc % 2, :], ps[0:HC, MISC, :], -1.0, None, ALU.mult)\
                    .then_inc(s_("misc_free"), 1)

            def q_low(chunk, cc):
                v.wait_ge(s_("q_rnd"), chunk + 1)
                dst = q0[R_LO:R_ROUND, cc]
                nc.vector.tensor_tensor(dst, fq[cc % 2][R_LO:R_ROUND], dst.bitcast(F32), ALU.subtract)\
                    .then_inc(s_("q_lo"), 1)

            def values(n, g):
                v.wait_ge(s_("misc_full"), n + 1)
                bias = bv0[:].rearrange("p (g h c) -> p g h c", g=2, c=HD)
                for k in range(5):
                    rows = NB if k == 4 else WAH
                    dst = v0[0:rows, g, k, :].rearrange("p (h n) -> p h n", h=HG)[:, :, 0:HD]
                    src = ps[0:rows, MISC, k * KC:(k + 1) * KC].rearrange("p (h c) -> p h c", c=HD)
                    last = nc.vector.tensor_tensor(dst, src, bias[0:rows, g], ALU.add)
                last.then_inc(s_("misc_free"), 1)

            def reciprocals(group, part):
                v.wait_ge(s_("os_ready"), group + 1)
                sums = osb[KC:KC + HG, part * (BT // 2):(part + 1) * (BT // 2)]
                nc.vector.reciprocal(sums, sums).then_inc(s_("rc_ready"), 1)

            def normalise(n, group, g):
                v.wait_ge(s_("misc_full"), n + 1)
                o4 = ot[:, g, :].rearrange("p (i y x) -> p i y x", i=2, y=SIDE)
                parts = [o4[:, :, 0:WS, 0:WS], o4[:, :, :, WS:SIDE], o4[:, :, WS:SIDE, 0:WS]]
                n0 = 2 * WA

                def cut(s):
                    rest = s[:, n0:BT].rearrange("p (i n) -> p i n", i=2)
                    return (s[:, 0:n0].rearrange("p (i y x) -> p i y x", i=2, x=WS),
                            rest[:, :, 0:NBD].rearrange("p i (y x) -> p i y x", x=SIDE - WS),
                            rest[:, :, NBD:NB1].rearrange("p i (y x) -> p i y x", x=WS))

                for o, s, r in zip(parts, cut(osb[0:KC]), cut(ps[0:KC, MISC, :])):
                    last = nc.vector.tensor_tensor(o, s, r, ALU.mult)
                last.then_inc(s_("misc_free"), 1)

            def residual(n, blk, half):
                v.wait_ge(s_("misc_full"), n + 1)
                xs = x_sb[:, bass.ds(blk * TPB + 2 * half, 2), :]
                nc.vector.tensor_tensor(xs, xs, ps[:, MISC, 0:2 * C].rearrange("p (t c) -> p t c", t=2), ALU.add)\
                    .then_inc(s_("misc_free"), 1)

            for u in range(2):
                last = nc.vector.memset(fq[u][32:64], 0.0)
            last.then_inc(s_("fq_zero"), 1)
            for k in range(5, 8):
                v.wait_ge(s_(f"stored{k}"), 16)
            v.wait_ge(s_("rel_out"), 16)
            nc.vector.memset(vpad, 0.0).then_inc(s_("vpad_zero"), 1)
            v.wait_ge(s_("vpad_zero"), 1)
            v.wait_ge(s_("v0_zero"), 1)
            v.wait_ge(s_("small_in"), 16 * 11)
            nc.vector.tensor_copy(vpad.rearrange("p g (h n) -> p g h n", h=HG)[:, :, :, 0:HD],
                                  bv0[:].rearrange("p (g h c) -> p g h c", g=2, c=HD))
            for h in range(HG):
                at = h * VW + HG * HD + h
                nc.vector.memset(v0[:, :, :, at:at + 1], 1.0)
                last = nc.vector.memset(vpad[0:NB, :, at:at + 1], 1.0)
            last.then_inc(s_("v_ones"), 1)
            q_low(0, 0)
            values(1, 0)
            q_low(1, 1)
            for c in range(2):
                for j in range(HC):
                    maxima(c, c, j)
                if c == 0:
                    minus(2, 0, 0)
                    q_low(2, 2)
            v.wait_ge(s_("x_bias"), BLKS)

            def body(blk, first, last):
                use = blk * 10
                for cc in range(CPB):
                    chunk = blk * CPB + cc
                    for j in range(HC):
                        if not (last and cc >= 2):
                            maxima(chunk + 2, (cc + 2) % CPB, j)
                        if j == 0 and not (last and cc == 3):
                            minus(tr_use(blk, cc, first), chunk + 1, (cc + 1) % CPB)
                        if cc == 0 and j < 2 and not first:
                            reciprocals(blk * 2 - 1, j)
                        if cc == 2 and j < 2:
                            reciprocals(blk * 2, j)
                        if j == 1 and not (last and cc >= 1):
                            q_low(chunk + 3, (cc + 3) % CPB)
                        if (cc, j) == (0, 2) and not first:
                            normalise(use + R1_, blk * 2 - 1, 1)
                        if (cc, j) == (1, 0) and not first:
                            residual(use + PA_, blk - 1, 0)
                            residual(use + PB_, blk - 1, 1)
                        if (cc, j) == (1, 1):
                            values(use + V1_, 1)
                        if (cc, j) == (2, 2):
                            normalise(use + R0_, blk * 2, 0)
                        if (cc, j) == (3, 1) and not last:
                            values(use + V0_, 0)

            peeled(v, body)
            ln_statistics(v, 1, 0)
            for part in range(2):
                reciprocals(2 * BLKS - 1, part)
            ln_normalise(v, 1, 0)
            use = BLKS * 10 - 2
            normalise(use, 2 * BLKS - 1, 1)
            residual(use + 1, BLKS - 1, 0)
            residual(use + 2, BLKS - 1, 1)
            v.wait_ge(s_("misc_free"), use + 3)

        def attn0_tensor(pe):
            mm = nc.tensor.matmul

            def scores_for_max(chunk, cc, j):
                if j == 0:
                    pe.wait_ge(s_("q_lo"), chunk + 1)
                    pe.wait_ge(s_("k_lo"), chunk + 1)
                pe.wait_ge(s_("max_done"), chunk * HC + j)
                q, k, p_ = q0[0:K_MAX, cc, j], k0[0:K_MAX, cc, j], pk[0:K_MAX, cc * HC + j]
                for i in range(2):
                    for c in range(2):
                        at = i * WA + c * WAH
                        mm(ps[0:WAH, SM_A + i, c * WA:(c + 1) * WA], q[:, at:at + WAH], k[:, i * WA:(i + 1) * WA],
                           start=True, stop=True)
                mm(ps[0:NB, SM_B, 0:NB], q[:, 2 * WA:BT], k[:, 2 * WA:BT], start=True, stop=True)
                mm(ps[0:NB, SM_B, NB:NB + PADS], q[:, 2 * WA:BT], p_, start=True, stop=True).then_inc(s_("sm_done"), 1)

            def scores(blk, cc, j):
                chunk = blk * CPB + cc
                if j == 0:
                    pe.wait_ge(s_(f"nm_in{cc % 2}"), (blk * 2 + cc // 2 + 1) * 16)
                pe.wait_ge(s_("exp_done"), chunk * HC + j)
                q, k, p_ = q0[0:R_MAX + 1, cc, j], k0[0:R_MAX + 1, cc, j], pk[0:R_MAX + 1, cc * HC + j]
                for i in range(2):
                    for c in range(2):
                        at = i * WA + c * WAH
                        mm(ps[0:WAH, ST_A + i, c * WA:(c + 1) * WA], k[:, at:at + WAH], q[:, i * WA:(i + 1) * WA],
                           start=True, stop=True)
                rhs = q[:, 2 * WA:BT]
                mm(ps[0:NB, ST_B, 0:NB], k[:, 2 * WA:BT], rhs, start=True, stop=True)
                for c in range(2):
                    last = mm(ps[0:NB, ST_B, (c + 1) * NB:(c + 2) * NB], p_[:, c * NB:(c + 1) * NB], rhs,
                              start=True, stop=True)
                last.then_inc(s_("st_done"), 1)

            def values_product(blk, cc, j):
                h = cc * HC + j
                n = blk * NH + h
                if cc % 2 == 0 and j == 0:
                    pe.wait_ge(s_("os_ready"), blk * 2 + cc // 2)
                pe.wait_ge(s_("exp_done"), n + 1)
                g, hh = h // HG, h % HG
                at = slice(hh * VW, (hh + 1) * VW)
                x, y = pa[h % 2], pb[h % 2]
                first = hh == 0
                for i in range(2):
                    for c in range(2):
                        mm(ps[0:VW, PV, i * WA:(i + 1) * WA], v0[0:WAH, g, 2 * i + c, at],
                           x[0:WAH, i, c * WA:(c + 1) * WA], start=first, stop=False, skip_group_check=True)
                        first = False
                for c in range(3):
                    vs = v0[0:NB, g, 4, at] if c == 0 else vpad[0:NB, g, at]
                    last = mm(ps[0:VW, PV, 2 * WA:BT], vs, y[0:NB, c], start=False, stop=hh == HG - 1 and c == 2,
                              skip_group_check=True)
                last.then_inc(s_("pv_done"), 1)

            def transposed_maxima(n, chunk, cc):
                pe.wait_ge(s_("misc_free"), n)
                pe.wait_ge(s_("max_done"), chunk * HC + HC)
                for k in range(4):
                    nc.tensor.transpose(ps[0:HC, MISC, k * WAH:(k + 1) * WAH], mxa[0:WAH, cc % 2, k, :],
                                        ident[0:WAH, 0:WAH])
                nc.tensor.transpose(ps[0:HC, MISC, 2 * WA:BT], mxb[0:NB, cc % 2, :], ident[0:NB, 0:NB])\
                    .then_inc(s_("misc_full"), 1)

            def values(n, blk, g):
                pe.wait_ge(s_("misc_free"), n)
                pe.wait_ge(s_("xp_ready"), blk + 1)
                for k in range(5):
                    rows = NB if k == 4 else WAH
                    for kc in range(2):
                        last = mm(ps[0:rows, MISC, k * KC:(k + 1) * KC], xp[:, kc, k * WAH:k * WAH + rows],
                                  wv0[:, kc, g * KC:(g + 1) * KC], start=kc == 0, stop=kc == 1)
                last.then_inc(s_("misc_full"), 1)

            def spread_reciprocals(n, group):
                pe.wait_ge(s_("misc_free"), n)
                pe.wait_ge(s_("rc_ready"), 2 * (group + 1))
                mm(ps[0:KC, MISC, :], CST["sel"][KC:KC + HG, :], osb[KC:KC + HG], start=True, stop=True)\
                    .then_inc(s_("misc_full"), 1)

            def projection(n, half):
                pe.wait_ge(s_("misc_free"), n)
                for u in range(2):
                    at = (2 * half + u) * P
                    for k in range(2):
                        last = mm(ps[:, MISC, u * C:(u + 1) * C], ot[:, k, at:at + P], wp[0][:, k, :],
                                  start=k == 0, stop=k == 1)
                last.then_inc(s_("misc_full"), 1)

            pe.wait_ge(s_("rows_set"), 2 * CPB)
            pe.wait_ge(s_("pk_ready"), 1)
            values(1, 0, 0)
            for c in range(2):
                for j in range(HC):
                    scores_for_max(c, c, j)
                if c == 0:
                    transposed_maxima(2, 0, 0)
            pe.wait_ge(s_("v_ones"), 1)

            def body(blk, first, last):
                use = blk * 10
                for cc in range(CPB):
                    chunk = blk * CPB + cc
                    for j in range(HC):
                        scores(blk, cc, j)
                        if not (last and cc >= 2):
                            scores_for_max(chunk + 2, (cc + 2) % CPB, j)
                        if cc or j:
                            values_product(blk, cc - (j == 0), (j - 1) % HC)
                        elif not first:
                            values_product(blk - 1, CPB - 1, HC - 1)
                        if j == 0 and not (last and cc == 3):
                            transposed_maxima(tr_use(blk, cc, first), chunk + 1, (cc + 1) % CPB)
                        if (cc, j) == (0, 2) and not first:
                            spread_reciprocals(use + R1_, blk * 2 - 1)
                        if (cc, j) == (1, 0) and not first:
                            projection(use + PA_, 0)
                            projection(use + PB_, 1)
                        if (cc, j) == (1, 1):
                            values(use + V1_, blk, 1)
                        if (cc, j) == (2, 2):
                            spread_reciprocals(use + R0_, blk * 2)
                        if (cc, j) == (3, 1) and not last:
                            values(use + V0_, blk + 1, 0)

            peeled(pe, body)
            values_product(BLKS - 1, CPB - 1, HC - 1)
            use = BLKS * 10 - 2
            spread_reciprocals(use, 2 * BLKS - 1)
            projection(use + 1, 0)
            projection(use + 2, 1)

        def attn0_scalar(act):
            def exponentials(blk, cc, j):
                h = cc * HC + j
                n = blk * NH + h
                act.wait_ge(s_("st_done"), n + 1)
                act.wait_ge(s_("pv_done"), n)
                nc.scalar.activation(pa[h % 2][0:WAH], ps[0:WAH, ST_A:ST_A + 2, 0:2 * WA], ACT.Exp)
                nc.scalar.activation(pb[h % 2][0:NB], ps[0:NB, ST_B, 0:3 * NB].rearrange("p (c n) -> p c n", c=3), ACT.Exp)\
                    .then_inc(s_("exp_done"), 1)

            def round_q(blk, n):
                cc = n % CPB
                act.wait_ge(s_(f"fq_in{n % 2}"), (blk * 2 + n // 2 + 1) * 64)
                nc.scalar.activation(q0[0:R_ROUND, cc], fq[cc % 2][0:R_ROUND], ACT.Copy).then_inc(s_("q_rnd"), 1)

            def round_k(blk, n):
                cc = n % CPB
                act.wait_ge(s_(f"fk_in{n % 2}"), (blk * 2 + n // 2 + 1) * 48)
                nc.scalar.activation(k0[0:R_ROUND, cc], fk[cc % 2][0:R_ROUND], ACT.Copy).then_inc(s_("k_rnd"), 1)

            def unnormalised(group, last_read):
                act.wait_ge(s_("misc_free"), last_read + 1)
                act.wait_ge(s_("pv_done"), group * HG + HG + 1)
                nc.scalar.activation(osb[0:VW], ps[0:VW, PV, :], ACT.Copy).then_inc(s_("os_ready"), 1)

            act.wait_ge(s_("rows_set"), 2 * CPB)
            for c in range(3):
                round_q(0, c)
                round_k(0, c)

            def body(blk, first, last):
                for cc in range(CPB):
                    chunk = blk * CPB + cc
                    for j in range(HC):
                        exponentials(blk, cc, j)
                        ahead = not (last and cc >= 1)
                        if (cc, j) == (0, 0) and not first:
                            unnormalised(blk * 2 - 1, (blk - 1) * 10 + R0_)
                        if (cc, j) == (2, 0):
                            unnormalised(blk * 2, blk * 10 + R1_)
                        if j == 0 and ahead:
                            round_q(blk, cc + 3)
                        if j == 1 and ahead:
                            round_k(blk, cc + 3)

            peeled(act, body)
            unnormalised(2 * BLKS - 1, (BLKS - 1) * 10 + R0_)

        LOGITS, RANKS, TOTALS, TABLES, LG = 4, 5, 6, 7, 5
        DOWN, XT = 6, 7
        TRIPS = MT // 3
        COLS = 2 * TILES

        def tripled(eng, body):
            for r in range(3):
                body(0, r, r == 0, False)
            with eng.Fori(1, TRIPS - 1) as trip:
                for r in range(3):
                    body(trip, r, False, False)
            for r in range(3):
                body(TRIPS - 1, r, False, True)

        rowhot = xnT[:, 0:COLS * P // 2].bitcast(BF16).rearrange("p (c n) -> p c n", c=COLS)
        ids = xnT[:, 2048:2048 + COLS * SLOTS].bitcast(BF16).rearrange("p (c k s) -> p c k s", c=COLS, k=2)
        tilehot = xnT[:, 3392:3392 + COLS * SLOTS // 2].bitcast(BF16).rearrange("p (c s) -> p c s", c=COLS)
        rowb = smallb[:, 0:COLS]
        tileb = smallb[:, COLS:2 * COLS]

        def numbers(ops, k):
            return ops.tensor_tensor(ids[:, :, k], tilehot, (idab, idbb)[k].unsqueeze(2).broadcast_to([P, COLS, SLOTS]),
                                     ALU.mult)

        def moe_sync(sp, l):
            if l == 0:
                sp.wait_ge(s_("misc_free"), 10 * BLKS + 1)
            else:
                sp.wait_ge(s_("y1_out"), 16 * 4 * len(DIL))
            for e in range(E):
                sp.dma_start(w1s[:, e], a[f"w1_{l}"][e]).then_inc(s_("w_in"), 16)
                if e < E - 2:
                    sp.dma_start(w2s[:, e], a[f"w2_{l}"][e]).then_inc(s_("w_in"), 16)
            for u in range(2):
                sp.wait_ge(s_(f"xn_kept{u}"), 16 * 2 * (l + 1))
            sp.wait_ge(s_("xn_free"), 2 + (2 + 2 * l) * BLKS)
            for e in range(E - 2, E):
                sp.dma_start(w2s[:, e], a[f"w2_{l}"][e]).then_inc(s_("w_in"), 16)
            sp.dma_start(b2s.rearrange("p e c -> p (e c)"), a[f"b2_{l}"]).then_inc(s_("w_in"), 16)
            for r in range(3):
                sp.wait_ge(s_(f"scattered{r}"), 16 * TRIPS * (l + 1))
            for b in range(BLKS):
                sp.dma_start(yt[:, b * TPB:(b + 1) * TPB],
                             yd[l].rearrange("(t p k) c -> p t k c", p=P, k=2)[:, b * TPB:(b + 1) * TPB])\
                    .then_inc(s_(f"y_in{b}"), 16)

        def moe_vector(v, l):
            vec = nc.vector
            at = [0]

            def tmp(*shape):
                n = 1
                for s in shape:
                    n *= s
                view = rt[:, at[0]:at[0] + n]
                at[0] += n
                if len(shape) > 1:
                    names = "abcd"[:len(shape)]
                    view = view.rearrange(f"p ({' '.join(names)}) -> p {' '.join(names)}",
                                          **dict(zip(names, shape)))
                return view

            logits, masked, shifted, place, ex = (tmp(TILES, E) for _ in range(5))
            hot = tmp(2, TILES, E)
            top, second, best, total, share = (tmp(TILES) for _ in range(5))
            scan = [tmp(COLS, E) for _ in range(2)]
            slot = tmp(COLS, E)
            counts, tiles, first_tile, base, end = (tmp(E) for _ in range(5))
            below = tmp(E, E)
            pos, row, tile_ = tmp(COLS), tmp(COLS), tmp(COLS)
            low, table, empty = tmp(SLOTS), tmp(SLOTS), tmp(SLOTS)
            over = tmp(SLOTS, E)
            hot_flat = hot.rearrange("p k t e -> p (k t) e")
            count = [l * ROUTE_STEPS[0]]

            def step(instruction):
                instruction.then_inc(s_("route"), 1)
                count[0] += 1
                v.wait_ge(s_("route"), count[0])

            def per_token(x):
                return x.unsqueeze(2).broadcast_to([P, TILES, E])

            def per_column(x):
                return x.unsqueeze(1).broadcast_to([P, COLS, E])

            rev = CST["rev"].unsqueeze(1).broadcast_to([P, TILES, E])
            ln_vector(v, 1 + 2 * l, (1,))
            v.wait_ge(s_("logits_mm"), (l + 1) * BLKS)
            step(vec.tensor_tensor(logits, ps[:, LOGITS, 0:TILES * E].rearrange("p (t e) -> p t e", e=E),
                                   bg[l][:].unsqueeze(1).broadcast_to([P, TILES, E]), ALU.add))
            for k, (src, value) in enumerate(((logits, top), (masked, second))):
                step(vec.tensor_reduce(value, src, AX.X, ALU.max))
                step(vec.tensor_tensor(place, src, per_token(value), ALU.is_equal))
                step(vec.tensor_tensor(place, place, rev, ALU.mult))
                step(vec.tensor_reduce(best, place, AX.X, ALU.max))
                step(vec.tensor_tensor(hot[:, k], place, per_token(best), ALU.is_equal))
                if k == 0:
                    vec.tensor_tensor(shifted, logits, per_token(top), ALU.subtract).then_inc(s_("shifted"), 1)
                    step(vec.scalar_tensor_tensor(masked, hot[:, 0], -1e30, logits, ALU.mult, ALU.add))
            vec.tensor_copy(hotb_v, hot_flat).then_inc(s_("hot_ready"), 1)
            v.wait_ge(s_("ranks_mm"), l + 1)
            totals = ps[:, TOTALS, 0:COLS * E].rearrange("p (c e) -> p c e", e=E)
            step(vec.tensor_copy(scan[0], totals))
            d, cur = 1, 0
            while d < COLS:
                vec.tensor_copy(scan[1 - cur][:, 0:d], scan[cur][:, 0:d])
                step(vec.tensor_tensor(scan[1 - cur][:, d:], scan[cur][:, d:], scan[cur][:, 0:COLS - d], ALU.add))
                d, cur = 2 * d, 1 - cur
            sums = scan[cur]
            step(vec.tensor_tensor(slot, sums, totals, ALU.subtract))
            step(vec.tensor_tensor(slot, slot, ps[:, RANKS, 0:COLS * E].rearrange("p (c e) -> p c e", e=E), ALU.add))
            step(vec.tensor_scalar(counts.bitcast(I32), sums[:, COLS - 1], float(P - 1), None, ALU.add))
            step(vec.tensor_scalar(counts.bitcast(I32), counts.bitcast(I32), 7, None, ALU.logical_shift_right))
            step(vec.tensor_copy(tiles, counts.bitcast(I32)))
            step(vec.tensor_tensor(below, CST["lt"].rearrange("p (a b) -> p a b", a=E),
                                   tiles.unsqueeze(1).broadcast_to([P, E, E]), ALU.mult))
            step(vec.tensor_reduce(first_tile, below, AX.X, ALU.add))
            vec.tensor_scalar(base, first_tile, float(P), None, ALU.mult)
            step(vec.tensor_tensor(end, first_tile, tiles, ALU.add))
            step(vec.tensor_tensor(slot, slot, per_column(base), ALU.add))
            step(vec.tensor_tensor(slot, slot, hot_flat, ALU.mult))
            step(vec.tensor_reduce(pos, slot, AX.X, ALU.add))
            step(vec.tensor_copy(row.bitcast(I32), pos))
            vec.tensor_scalar(tile_.bitcast(I32), row.bitcast(I32), 7, None, ALU.logical_shift_right)
            step(vec.tensor_scalar(pos.bitcast(I32), row.bitcast(I32), P - 1, None, ALU.bitwise_and))
            vec.tensor_copy(rowb, pos.bitcast(I32))
            vec.tensor_copy(tileb, tile_.bitcast(I32)).then_inc(s_("rows_ready"), 1)
            v.wait_ge(s_("rows_ready"), l + 1)
            vec.tensor_tensor(tilehot, iotsb.unsqueeze(1).broadcast_to([P, COLS, SLOTS]),
                              tileb.unsqueeze(2).broadcast_to([P, COLS, SLOTS]), ALU.is_equal)\
                .then_inc(s_("tilehot_ready"), 1)
            vec.tensor_tensor(rowhot, iotb.unsqueeze(1).broadcast_to([P, COLS, P]),
                              rowb.unsqueeze(2).broadcast_to([P, COLS, P]), ALU.is_equal)
            v.wait_ge(s_("tilehot_ready"), l + 1)
            numbers(vec, 0).then_inc(s_("ids_ready"), 1)
            step(vec.tensor_tensor(over[0:1], CST["iots"][0:1].unsqueeze(2).broadcast_to([1, SLOTS, E]),
                                   end[0:1].unsqueeze(1).broadcast_to([1, SLOTS, E]), ALU.is_ge))
            step(vec.tensor_reduce(low[0:1], over[0:1], AX.X, ALU.add))
            vec.tensor_scalar(te[:], low[0:1], float(E - 1), None, ALU.min).then_inc(s_("te_ready"), 1)
            v.wait_ge(s_("te_ready"), l + 1)
            v.wait_ge(s_("tables_mm"), l + 1)
            step(vec.tensor_copy(low, ps[:, TABLES, SLOTS:2 * SLOTS]))
            step(vec.scalar_tensor_tensor(table, ps[:, TABLES, 0:SLOTS], 64.0, low, ALU.mult, ALU.add))
            step(vec.tensor_scalar(empty, table, 0.0, 4.0 * T, ALU.is_equal, ALU.mult))
            vec.tensor_scalar(low.bitcast(I32), table, -1.0, 0.0, ALU.add, ALU.max)
            step(vec.tensor_scalar(table, table, -1.0, None, ALU.add))
            step(vec.tensor_tensor(sidx[:], table, empty, ALU.add))
            vec.memset(xgT[KC:KC + 1, 0], 1.0)
            step(vec.tensor_scalar(gidx[:], low.bitcast(I32), 1, None, ALU.logical_shift_right))
            vec.memset(credit[0:1, 7:8], 0.0).then_inc(s_("routed"), 1)
            v.wait_ge(s_("exp_gates"), l + 1)
            step(vec.tensor_reduce(total, ex, AX.X, ALU.add))
            step(vec.reciprocal(gw[:, 0], total))
            step(vec.tensor_tensor(place, ex, hot[:, 1], ALU.mult))
            step(vec.tensor_reduce(share, place, AX.X, ALU.add))
            step(vec.tensor_tensor(gw[:, 1], share, gw[:, 0], ALU.mult))
            if l == 1:
                step(vec.tensor_tensor(total, gw[:, 0], gw[:, 1], ALU.add))
                step(vec.tensor_scalar(total, total, 1e-9, None, ALU.add))
                step(vec.reciprocal(total, total))
                step(vec.tensor_tensor(gw[:], gw[:], total.unsqueeze(1).broadcast_to([P, 2, TILES]), ALU.mult))
            ROUTE_STEPS[0] = count[0] if l == 0 else ROUTE_STEPS[0]

            n0 = l * MT

            def gathered(n):
                v.wait_ge(s_("trx_done"), n + 1)
                vec.tensor_copy(xgT[0:KC], ps[0:KC, XT, 0:2 * P].rearrange("p (k n) -> p k n", k=2))\
                    .then_inc(s_("xgT_ready"), 1)

            def result(n, trip, r):
                e = v.value_load(te[0:1, bass.ds(n - n0, 1)], min_val=0, max_val=E - 1)
                v.wait_ge(s_("down_done"), n + 1)
                v.wait_ge(s_(f"scattered{r}"), (trip + l * TRIPS) * 16)
                vec.tensor_tensor(ys[r], ps[:, DOWN, 0:C], b2s[:, e, :], ALU.add).then_inc(s_("y_ready"), 1)

            def expert_weights(n, trip, r, wait=True):
                e = v.value_load(te[0:1, bass.ds(n - n0, 1)], min_val=0, max_val=E - 1)
                if wait:
                    v.wait_ge(s_("up_done"), n - 2)
                for k in range(2):
                    last = vec.tensor_copy(wcur[r][k][0:KC + 1 - k], w1s[0:KC + 1 - k, e, k, :])
                last.then_inc(s_("wcur_ready"), 1)

            def body(trip, r, first, last):
                n = n0 + trip * 3 + r
                if not (last and r >= 1):
                    expert_weights(n + 2, trip + (r > 0), (r + 2) % 3, not (first and r == 0))
                if not (last and r == 2):
                    gathered(n + 1)
                if not (first and r == 0):
                    result(n - 1, trip - (r == 0), (r - 1) % 3)

            v.wait_ge(s_("w_in"), 16 * 17 * (l + 1))
            for r in range(2):
                expert_weights(n0 + r, 0, r, False)
            gathered(n0)
            tripled(v, body)
            result(n0 + MT - 1, TRIPS - 1, 2)
            for b in range(BLKS):
                v.wait_ge(s_(f"y_in{b}"), 16 * (l + 1))
                for k in range(2):
                    if k:
                        v.wait_ge(s_("first_added"), l * BLKS + b + 1)
                    for t in range(b * TPB, (b + 1) * TPB):
                        last = vec.scalar_tensor_tensor(x_sb[:, t], yt[:, t, k], gw[:, k, t:t + 1], x_sb[:, t],
                                                        ALU.mult, ALU.add)
                    last.then_inc(s_("combined" if k else "first_added"), 1)
                if l == 0 and b % 2:
                    v.wait_ge(s_("combined"), b + 1)
                    ln_vector(v, 2, (b // 2,))

        def moe_tensor(pe, l):
            n0 = l * MT
            mm = nc.tensor.matmul
            for turn in range(2):
                blocks = (2 * turn, 2 * turn + 1)
                for b in blocks:
                    ln_transpose(pe, 1 + 2 * l, b, b % 2)
                for b in blocks:
                    pe.wait_ge(s_("tp_free"), xnT_at(1 + 2 * l, b))
                    if turn:
                        pe.wait_ge(s_("lg_out"), l * BLKS + b - 1)
                    for k in range(2):
                        last = mm(ps[0:E, LG + b % 2, :], wg[l][:, k, :], xnT_v[:, k, b * BT:(b + 1) * BT],
                                  start=k == 0, stop=k == 1)
                    last.then_inc(s_("lg_mm"), 1)
                for b in blocks:
                    pe.wait_ge(s_("lg_out"), l * BLKS + b + 1)
                    for j in range(TPB):
                        t = b * TPB + j
                        last = nc.tensor.transpose(ps[:, LOGITS, t * E:(t + 1) * E], lg[:, b % 2, j * P:(j + 1) * P],
                                                   ident[0:E, 0:E])
                    last.then_inc(s_("logits_mm"), 1)
            pe.wait_ge(s_("hot_ready"), l + 1)
            flat = hotb_v.rearrange("p c e -> p (c e)")
            mm(ps[:, RANKS, 0:COLS * E], trib, flat, start=True, stop=True)
            mm(ps[:, TOTALS, 0:COLS * E], onesb, flat, start=True, stop=True).then_inc(s_("ranks_mm"), 1)
            pe.wait_ge(s_("ids_ready"), l + 1)
            pe.wait_ge(s_("ids_pool"), l + 1)
            for c in range(COLS):
                last = mm(ps[:, TABLES, 0:2 * SLOTS], rowhot[:, c], ids[:, c].rearrange("p k s -> p (k s)"),
                          start=c == 0, stop=c == COLS - 1)
            last.then_inc(s_("tables_mm"), 1)

            def gathered(n, trip, r):
                pe.wait_ge(s_(f"gathered{r}"), (trip + 1 + l * TRIPS) * 16)
                pe.wait_ge(s_("xgT_ready"), n)
                for k in range(2):
                    last = nc.tensor.transpose(ps[0:KC, XT, k * P:(k + 1) * P], xg[r][:, k * KC:(k + 1) * KC], ident)
                last.then_inc(s_("trx_done"), 1)

            def down(n):
                e = pe.value_load(te[0:1, bass.ds(n - n0, 1)], min_val=0, max_val=E - 1)
                pe.wait_ge(s_("hid_ready"), n + 1)
                pe.wait_ge(s_("y_ready"), n)
                for f in range(FT):
                    last = mm(ps[:, DOWN, 0:C], hidT[:, f, :], w2s[:, e, f, :], start=f == 0, stop=f == FT - 1)
                last.then_inc(s_("down_done"), 1)

            def body(trip, r, first, last_):
                n = n0 + trip * 3 + r
                pe.wait_ge(s_("xgT_ready"), n + 1)
                pe.wait_ge(s_("wcur_ready"), n + 1)
                for f in range(FT):
                    for k in range(2):
                        rows = KC + 1 - k
                        last = mm(ps[:, 2 * r + f // 4, f % 4 * P:(f % 4 + 1) * P],
                                  wcur[r][k][0:rows, f * P:(f + 1) * P], xgT[0:rows, k, :], start=k == 0, stop=k == 1)
                last.then_inc(s_("up_done"), 1)
                if not (last_ and r == 2):
                    gathered(n + 1, trip + (r == 2), (r + 1) % 3)
                if not (first and r == 0):
                    down(n - 1)

            pe.wait_ge(s_("w_in"), 16 * 17 * (l + 1))
            pe.wait_ge(s_("te_ready"), l + 1)
            gathered(n0, 0, 0)
            tripled(pe, body)
            down(n0 + MT - 1)

        def copy_logits(act, l, b):
            act.wait_ge(s_("lg_mm"), l * BLKS + b + 1)
            if b >= 2:
                act.wait_ge(s_("logits_mm"), l * BLKS + b - 1)
            nc.scalar.activation(lg[:, b % 2, :], ps[0:E, LG + b % 2, :], ACT.Copy).then_inc(s_("lg_out"), 1)

        def moe_scalar(act, l):
            banks = ps[:].rearrange("p b n -> p (b n)")
            n = 1 + 2 * l
            ln_root(act, n, 0)
            ln_copy(act, n, 0)
            ln_copy(act, n, 1)
            ln_root(act, n, 1)
            for b in (0, 1):
                copy_logits(act, l, b)
            ln_copy(act, n, 2)
            ln_copy(act, n, 3)
            for b in (2, 3):
                copy_logits(act, l, b)
            act.wait_ge(s_("shifted"), l + 1)
            nc.scalar.activation(rt[:, 4 * TILES * E:5 * TILES * E], rt[:, 2 * TILES * E:3 * TILES * E], ACT.Exp)\
                .then_inc(s_("exp_gates"), 1)

            def body(trip, r, first, last):
                n = l * MT + trip * 3 + r
                act.wait_ge(s_("up_done"), n + 1)
                act.wait_ge(s_("down_done"), n)
                nc.scalar.activation(hidT.rearrange("p f n -> p (f n)"), banks[:, 2 * r * 512:2 * r * 512 + F], ACT.Gelu)\
                    .then_inc(s_("hid_ready"), 1)

            tripled(act, body)

        def moe_pool(pool, l):
            def held(kind, before):
                pool.wait_ge(s_(f"held{kind}"), before)
                nc.gpsimd.tensor_tensor(credit[0:1, 12 + kind:13 + kind], credit[0:1, 0:1], credit[0:1, 0:1], ALU.add)\
                    .then_inc(s_(f"held{kind}"), 1)

            def gather(n, r):
                nc.gpsimd.tensor_copy(gcur[:, r:r + 1], gidx[:, bass.ds(n - n0, 1)]).then_inc(s_("gcur_ready"), 1)
                pool.wait_ge(s_("gcur_ready"), n + 1)
                held(1, n)
                nc.gpsimd.indirect_dma_start(out=xg[r], out_offset=None, in_=xnd[l],
                                             in_offset=bass.IndirectOffsetOnAxis(ap=gcur[:, r:r + 1], axis=0))\
                    .then_inc(s_(f"gathered{r}"), 16)

            def scatter(n, r):
                pool.wait_ge(s_("y_ready"), n + 1)
                held(2, n)
                nc.gpsimd.tensor_copy(scur[:, r:r + 1], sidx[:, bass.ds(n - n0, 1)]).then_inc(s_("scur_ready"), 1)
                pool.wait_ge(s_("scur_ready"), n + 1)
                held(3, n)
                nc.gpsimd.indirect_dma_start(out=yd[l], out_offset=bass.IndirectOffsetOnAxis(ap=scur[:, r:r + 1], axis=0),
                                             in_=ys[r], in_offset=None, bounds_check=2 * T - 1, oob_is_err=False)\
                    .then_inc(s_(f"scattered{r}"), 16)

            n0 = l * MT
            for b in range(BLKS):
                pool.wait_ge(s_("xn_ready"), (1 + 2 * l) * BLKS + b + 1)
                pool.dma_start(xnd[l][b * BT:(b + 1) * BT].rearrange("(t p) c -> p t c", p=P),
                               normed(1, b))\
                    .then_inc(s_(f"xn_kept{b % 2}"), 16)
            pool.wait_ge(s_("tilehot_ready"), l + 1)
            numbers(nc.gpsimd, 1).then_inc(s_("ids_pool"), 1)
            for u in range(2):
                pool.wait_ge(s_(f"xn_kept{u}"), 16 * 2 * (l + 1))
            pool.wait_ge(s_("routed"), l + 1)
            for r in range(3):
                gather(n0 + r, r)

            def body(trip, r, first, last):
                n = n0 + trip * 3 + r
                if not last:
                    pool.wait_ge(s_("trx_done"), n + 1)
                    held(0, n - l * 3)
                    gather(n + 3, r)
                if not first:
                    scatter(n - 1, (r - 1) % 3)

            tripled(pool, body)
            scatter(n0 + MT - 1, 2)

        QR = SIDE // 4
        SLOTS1 = 10
        QKV_STEPS = 24
        QPIX = QR * SIDE
        NEIGH = [(dy, dx) for dx in (0, -1, 1) for dy in (-1, 0, 1)]
        NN = len(NEIGH)

        def halo(d):
            return QR + 2 * d

        def columns(d, dx):
            return max(0, -dx * d), SIDE - d * abs(dx)

        k1, v1 = [], []
        at1 = 0
        for views in (k1, v1):
            for d in DIL:
                views.append(ar(at1, [HD, halo(d), SIDE]))
                at1 += HD * halo(d) * SIDE
        halos = at1
        q1 = [ar(at1 + i * HD * QPIX, [HD, QR, SIDE]) for i in range(3)]
        at1 += 3 * HD * QPIX
        stage = ar(at1, [SLOTS1, 2, PIX], KC)
        acc = [ar(at1 + i * QPIX * HD, [QPIX * HD]) for i in range(3)]
        prod = [xn[:, :, :, :].rearrange("p u t c -> p (u t c)")[:, 0:HD * QPIX], ar(at1 + SLOTS1 * BT, [HD * QPIX]),
                xt_(2 * HD * QPIX, [HD * QPIX]), xt_(3 * HD * QPIX, [HD * QPIX])]
        yl = xt_(0, [TILES, C])
        sc = [rt[:, i * NN * QPIX:(i + 1) * NN * QPIX] for i in range(3)]
        mx1 = rt[:, 3 * NN * QPIX:3 * NN * QPIX + QPIX]
        sm1 = [rt[:, 3 * NN * QPIX + (1 + i) * QPIX:3 * NN * QPIX + (2 + i) * QPIX] for i in range(3)]
        yT = [rt[0:KC, u * 2 * BT:(u + 1) * 2 * BT].rearrange("p (k n) -> p k n", k=2) for u in range(2)]

        def store_qkv(eng, pool, phase):
            for t in range(phase * 8, phase * 8 + 8):
                image, u, pair = t // 12, t % 12 // 2, t % 2
                for g in range(2):
                    if ((2 * t + g) % 3 == 2) != pool:
                        continue
                    n = image * 36 + u * 6
                    eng.wait_ge(s_("qkv_staged"), t + 3)
                    eng.dma_start(qkvd[n:n + 6, 2 * pair + g], stage[:, t % SLOTS1, g])\
                        .then_inc(s_(f"qkv_out{int(pool)}{phase}"), 16)

        def wait_for_qkv(eng, phase):
            by_pool = sum(k % 3 == 2 for k in range(phase * 16, phase * 16 + 16))
            eng.wait_ge(s_(f"qkv_out0{phase}"), 16 * (16 - by_pool))
            eng.wait_ge(s_(f"qkv_out1{phase}"), 16 * by_pool)

        def attn1_sync(sp):
            def load(i):
                d = DIL[i]
                for t, name, dst in ((0, "qk", q1), (1, "qk", k1), (2, "v", v1)):
                    n = (i * 3 + t) * SPU
                    src = qkvd[n:n + SPU].rearrange("b g c x -> (b g) c x")
                    edge = d if t else 0
                    for quarter in range(4):
                        lo = max(0, quarter * QR - edge)
                        hi = min(SIDE, (quarter + 1) * QR + edge)
                        row = lo - (quarter * QR - edge)
                        to = dst[i][quarter * 32:(quarter + 1) * 32, :, row:row + hi - lo, :]
                        sp.dma_start(to.rearrange("p c y x -> p c (y x)"), src[:, :, lo * SIDE:hi * SIDE])\
                            .then_inc(s_(f"{name}_in{i}"), 16)

            store_qkv(sp, False, 0)
            store_qkv(sp, False, 1)
            sp.wait_ge(s_("halo_zero"), 2)
            wait_for_qkv(sp, 0)
            load(0)
            store_qkv(sp, False, 2)
            for i in (1, 2):
                wait_for_qkv(sp, i)
                load(i)
            for i in range(3):
                sp.wait_ge(s_("acc_ready"), i + 1)
                for quarter in range(4):
                    dst = y1d.rearrange("(g i b) (q n) c -> i q b g (n c)", i=3, b=SPU, q=4)[i, quarter]
                    sp.dma_start(dst, acc[i][quarter * 32:(quarter + 1) * 32]).then_inc(s_("y1_out"), 16)
            sp.wait_ge(s_("y1_out"), 16 * 12)
            flat = y1d.rearrange("s n c -> (s n c)").rearrange("(t p c) -> p t c", p=P, c=C)
            for b in range(BLKS):
                sp.dma_start(yl[:, b * TPB:(b + 1) * TPB], flat[:, b * TPB:(b + 1) * TPB])\
                    .then_inc(s_(f"yl_in{b}"), 16)

        def attn1_pool(pool):
            pool.wait_ge(s_("y_ready"), MT)
            nc.gpsimd.memset(ar(halos // 2, [halos // 2]), 0.0).then_inc(s_("halo_zero"), 1)
            pool.wait_ge(s_("combined"), BLKS)
            nc.gpsimd.memset(ar(0, [halos // 2]), 0.0).then_inc(s_("halo_zero"), 1)
            for phase in range(3):
                store_qkv(pool, True, phase)
            pool.wait_ge(s_("halo_zero"), 2)
            pool.wait_ge(s_("xn_ready"), 3 * BLKS)
            for b in range(BLKS):
                xs = x_sb[:, b * TPB:(b + 1) * TPB, :]
                nc.gpsimd.tensor_tensor(xs, xs, bp[1][:].unsqueeze(1).broadcast_to([P, TPB, C]), ALU.add)\
                    .then_inc(s_("x_bias"), 1)
            for i in range(3):
                pool_values(pool, i)

        def value_product(ops, i, n, to):
            (dy, dx), d = NEIGH[n], DIL[i]
            x0, w = columns(d, dx)
            o = to.rearrange("p (y x c) -> p y x c", c=HD, x=SIDE)[:, :, x0:x0 + w, :]
            weight = sc[i][:, n * QPIX:(n + 1) * QPIX].rearrange("p (y x) -> p y x", x=SIDE)[:, :, x0:x0 + w]
            val = v1[i][:, :, d + dy * d:d + dy * d + QR, x0 + dx * d:x0 + dx * d + w]
            return ops.tensor_tensor(o, val.rearrange("p c y x -> p y x c"),
                                     weight.unsqueeze(3).broadcast_to([P, QR, w, HD]), ALU.mult)

        def pool_values(pool, i):
            pool.wait_ge(s_("norm"), 3 * (i + 1))
            pool.wait_ge(s_(f"v_in{i}"), 4 * 16)
            for n in range(NN):
                m = i * NN + n
                if i < 2:
                    if m >= 2:
                        pool.wait_ge(s_("pv_sum"), m - 1)
                    value_product(nc.gpsimd, i, n, prod[2 + m % 2]).then_inc(s_("pv_pool"), 1)
                elif n % 3 == 2:
                    pool.wait_ge(s_("pv_sum"), 2 * NN + n // 3 * 2)
                    value_product(nc.gpsimd, i, n, prod[3]).then_inc(s_("pv_pool"), 1)

        def vector_values(v):
            v.wait_ge(s_("v_in2"), 4 * 16)
            for col in range(3):
                to = prod[0 if col % 2 == 0 else 2]
                if col:
                    v.wait_ge(s_("pv_sum"), 2 * NN + col - 1)
                    v.wait_ge(s_("pv_vector"), col)
                value_product(nc.vector, 2, 3 * col, to).then_inc(s_("pair"), 1)
                value_product(nc.vector, 2, 3 * col + 1, prod[1]).then_inc(s_("pair"), 1)
                v.wait_ge(s_("pair"), 2 * col + 2)
                x0, w = columns(DIL[2], NEIGH[3 * col][1])
                a_, b_ = (t.rearrange("p (y x) -> p y x", y=QR)[:, :, x0 * HD:(x0 + w) * HD] for t in (to, prod[1]))
                nc.vector.tensor_tensor(a_, a_, b_, ALU.add).then_inc(s_("pv_vector"), 1)

        def attn1_vector(v):
            def product(i, n):
                d, (dy, dx) = DIL[i], NEIGH[n]
                x0, w = columns(d, dx)
                o = prod[n % 2].rearrange("p (c y x) -> p c y x", c=HD, x=SIDE)[:, :, :, x0:x0 + w]
                key = k1[i][:, :, d + dy * d:d + dy * d + QR, x0 + dx * d:x0 + dx * d + w]
                if n >= 2 or i:
                    v.wait_ge(s_("qk_sum"), i * NN + n - 1)
                nc.vector.tensor_tensor(o, q1[i][:, :, :, x0:x0 + w], key, ALU.mult).then_inc(s_("qk_prod"), 1)

            def channel_sum(i, n):
                x0, w = columns(DIL[i], NEIGH[n][1])
                src = prod[n % 2].rearrange("p (c y x) -> p y x c", c=HD, x=SIDE)[:, :, x0:x0 + w, :]
                o = sc[i][:, n * QPIX:(n + 1) * QPIX].rearrange("p (y x) -> p y x", x=SIDE)[:, :, x0:x0 + w]
                v.wait_ge(s_("qk_prod"), i * NN + n + 1)
                nc.vector.tensor_reduce(o, src, AX.X, ALU.add).then_inc(s_("qk_sum"), 1)

            def by_neighbour(s):
                return s.rearrange("p (n x) -> p n x", n=NN)

            def scores(i):
                v.wait_ge(s_(f"qk_in{i}"), 8 * 16)
                for n in range(NN + 1):
                    if n < NN:
                        product(i, n)
                    if n:
                        channel_sum(i, n - 1)
                v.wait_ge(s_("qk_sum"), (i + 1) * NN)
                nc.vector.tensor_reduce(mx1, sc[i].rearrange("p (n x) -> p x n", n=NN), AX.X, ALU.max)\
                    .then_inc(s_("soft"), 1)
                v.wait_ge(s_("soft"), i + 1)
                nc.vector.tensor_tensor(by_neighbour(sc[i]), by_neighbour(sc[i]),
                                        mx1.unsqueeze(1).broadcast_to([P, NN, QPIX]), ALU.subtract)\
                    .then_inc(s_("sc_ready"), 1)

            def weights(i):
                v.wait_ge(s_("ex_ready"), i + 1)
                nc.vector.tensor_reduce(sm1[i], sc[i].rearrange("p (n x) -> p x n", n=NN), AX.X, ALU.add)\
                    .then_inc(s_("norm"), 1)
                v.wait_ge(s_("norm"), 3 * i + 1)
                nc.vector.reciprocal(sm1[i], sm1[i]).then_inc(s_("norm"), 1)
                v.wait_ge(s_("norm"), 3 * i + 2)
                nc.vector.tensor_tensor(by_neighbour(sc[i]), by_neighbour(sc[i]),
                                        sm1[i].unsqueeze(1).broadcast_to([P, NN, QPIX]), ALU.mult)\
                    .then_inc(s_("norm"), 1)
                v.wait_ge(s_("norm"), 3 * i + 3)

            nc.vector.memset(rt[:, 0:3 * NN * QPIX], 0.0).then_inc(s_("sc_zero"), 1)
            v.wait_ge(s_("sc_zero"), 1)
            for i in range(3):
                scores(i)
                weights(i)
            vector_values(v)
            v.wait_ge(s_("x_bias"), 2 * BLKS)
            for b in range(BLKS):
                v.wait_ge(s_("proj1_mm"), b + 1)
                xs = x_sb[:, b * TPB:(b + 1) * TPB, :].rearrange("p (h t) c -> p h t c", h=2)
                u = b % 2 * 2
                nc.vector.tensor_tensor(xs, xs, ps[:, u:u + 2, 0:2 * C].rearrange("p h (t c) -> p h t c", t=2), ALU.add)\
                    .then_inc(s_("proj1_out"), 1)
                if b % 2:
                    v.wait_ge(s_("proj1_out"), b + 1)
                    if b == 1:
                        ln_vector(v, 3, (0,))

        def attn1_tensor(pe):
            ln_tensor(pe, 2)
            with pe.Fori(0, 2) as image:
                for u in range(6):
                    for pair in range(2):
                        pe.wait_ge(s_("tp_free"), xnT_at(2, 2 * pair + 1))
                        pe.wait_ge(s_("qkv_staged"), image * 12 + u * 2 + pair + 1)
                        for g in range(2):
                            last = nc.tensor.matmul(ps[0:KC, 4 + pair, g * PIX:(g + 1) * PIX], wqkv1[:, u % 3, :],
                                                    xnT_v[:, u // 3, bass.ds((2 * pair + g) * BT + image * PIX, PIX)],
                                                    start=True, stop=True)
                        last.then_inc(s_("qkv_mm"), 1)
            def add_product(i, dx, source, first, last_):
                x0, w = columns(DIL[i], dx)
                for half in range(2):
                    src = source.rearrange("p (h y n) -> p h y n", h=2, y=2)[:, half, :, x0 * HD:(x0 + w) * HD]
                    dst = ps[:, i % 2 * 2 + half, :].rearrange("p (y n) -> p y n", y=2)[:, :, x0 * HD:(x0 + w) * HD]
                    last = nc.tensor.matmul(dst, ident, src, start=first, stop=last_, skip_group_check=True)
                last.then_inc(s_("pv_sum"), 1)

            for i in range(2):
                for n, (dy, dx) in enumerate(NEIGH):
                    m = i * NN + n
                    pe.wait_ge(s_("pv_pool"), m + 1)
                    add_product(i, dx, prod[2 + m % 2], n == 0, n == NN - 1)
            pe.wait_ge(s_("acc_ready"), 1)
            for col in range(3):
                dx = NEIGH[3 * col][1]
                pe.wait_ge(s_("pv_vector"), col + 1)
                add_product(2, dx, prod[0 if col % 2 == 0 else 2], col == 0, False)
                pe.wait_ge(s_("pv_pool"), 2 * NN + col + 1)
                add_product(2, dx, prod[3], False, col == 2)

            def transpose(b):
                pe.wait_ge(s_(f"yl_in{b}"), 16)
                if b >= 2:
                    pe.wait_ge(s_("yT_ready"), b - 1)
                for k in range(2):
                    for j in range(TPB):
                        last = nc.tensor.transpose(ps[0:KC, 4 + b % 2 * 2 + k, j * P:(j + 1) * P],
                                                   yl[:, b * TPB + j, k * KC:(k + 1) * KC], ident)
                last.then_inc(s_("yl_mm"), 1)

            def project(b):
                pe.wait_ge(s_("yT_ready"), b + 1)
                pe.wait_ge(s_("acc_ready"), 3)
                if b >= 2:
                    pe.wait_ge(s_("proj1_out"), b - 1)
                for j in range(TPB):
                    for k in range(2):
                        last = nc.tensor.matmul(ps[:, b % 2 * 2 + j // 2, j % 2 * C:(j % 2 + 1) * C],
                                                yT[b % 2][:, k, j * P:(j + 1) * P], wp[1][:, k, :],
                                                start=k == 0, stop=k == 1)
                last.then_inc(s_("proj1_mm"), 1)

            for b in range(BLKS + 1):
                if b < BLKS:
                    transpose(b)
                if b:
                    project(b - 1)
            pe.wait_ge(s_("proj1_out"), BLKS)

        def attn1_scalar(act):
            ln_scalar(act, 2)
            for t in range(QKV_STEPS):
                if t in (SLOTS1, SLOTS1 + 8):
                    wait_for_qkv(act, 0 if t == SLOTS1 else 1)
                act.wait_ge(s_("qkv_mm"), t + 1)
                nc.scalar.activation(stage[:, t % SLOTS1].rearrange("p g n -> p (g n)"), ps[0:KC, 4 + t % 2, :], ACT.Copy)\
                    .then_inc(s_("qkv_staged"), 1)
            wait_for_qkv(act, 2)
            for i in range(3):
                act.wait_ge(s_("sc_ready"), i + 1)
                nc.scalar.activation(sc[i], sc[i], ACT.Exp, scale=HD ** -0.5).then_inc(s_("ex_ready"), 1)
                if i:
                    value_sums(act, i - 1)
            value_sums(act, 2)
            for b in range(BLKS):
                act.wait_ge(s_("yl_mm"), b + 1)
                if b >= 2:
                    act.wait_ge(s_("proj1_mm"), b - 1)
                u = 4 + b % 2 * 2
                nc.scalar.activation(yT[b % 2], ps[0:KC, u:u + 2, :], ACT.Copy).then_inc(s_("yT_ready"), 1)

        def value_sums(act, i):
            act.wait_ge(s_("pv_sum"), (i + 1) * NN if i < 2 else 2 * NN + 6)
            u = i % 2 * 2
            nc.scalar.activation(acc[i].rearrange("p (h n) -> p h n", h=2), ps[:, u:u + 2, :], ACT.Copy)\
                .then_inc(s_("acc_ready"), 1)
        @block.sync
        def _(sp):
            sp.dma_start(cq[KC:R_MAX + 1], a["cq"][KC:R_MAX + 1]).then_inc(s_("cqk_in"), 16)
            sp.dma_start(ck, a["ck"]).then_inc(s_("cqk_in"), 16)
            for b in range(BLKS):
                sp.dma_start(x_sb[:, b * TPB:(b + 1) * TPB, :],
                             a["x"].rearrange("(t p) c -> p t c", p=P)[:, b * TPB:(b + 1) * TPB, :])\
                    .then_inc(s_(f"x_in{b}"), 16)
            sp.dma_start(cst[:], a["cst"]).then_inc(s_("cst_in"), 16)
            sp.dma_start(wqk0[:], a["wqk0"]).then_inc(s_("wqk_in"), 16)
            sp.dma_start(bqk0[:], a["bqk0"]).then_inc(s_("wqk_in"), 16)
            sp.dma_start(padf, a["cpad"].unsqueeze(1).broadcast_to([P, NH, PADS])).then_inc(s_("padf_in"), 16)
            for i, name in enumerate(("relh", "relw")):
                sp.dma_start(relt[i], a[name]).then_inc(s_("rel_in"), 16)
            small = [(wv0, "wv0"), (bv0, "bv0"), (wqkv1, "wqkv1")]
            for l in range(2):
                small += [(wp[l], f"wp{l}"), (bp[l], f"bp{l}"), (wg[l], f"wg{l}"), (bg[l], f"bg{l}")]
            for t, name in small:
                sp.dma_start(t[:], a[name]).then_inc(s_("small_in"), 16)
            sp.wait_ge(s_("kps_ready"), 2)
            for g in range(2):
                sp.dma_start(kpd[g * HG:(g + 1) * HG].rearrange("h c n -> (h c) n"), kps[:, g, :])\
                    .then_inc(s_("kpd_out"), 16)
            sp.wait_ge(s_("kpd_out"), 32)
            sp.wait_ge(s_("padf_in"), 16)
            for r in (R_HI, R_DUP, R_LO):
                sp.dma_start(padf[r:r + HD], kpd.rearrange("h c n -> c h n")).then_inc(s_("padf_in"), 16)
            for k in range(8):
                if k < 2:
                    sp.wait_ge(s_("k_free"), 2 + 2 * BLKS)
                else:
                    sp.wait_ge(s_("staged"), k - 1)
                g, src = k % 2, pt[k % 3]
                hs = slice(g * HG, (g + 1) * HG)
                if k < 2:
                    dst, rows = kd[hs], KC
                elif k < 4:
                    dst, rows = qd[hs, 0:HD], KC
                else:
                    r = HD + WS * (k // 2 - 2)
                    dst, rows = qd[hs, r:r + WS], HG * WS
                sp.dma_start(dst, src[0:rows]).then_inc(s_(f"stored{k}"), 16)
            sp.wait_ge(s_("small_in"), 16 * 11)
            attn0_sync(sp)
            moe_sync(sp, 0)
            attn1_sync(sp)
            moe_sync(sp, 1)
            for b in range(BLKS):
                sp.wait_ge(s_("combined"), BLKS + b + 1)
                sp.dma_start(out[b * BT:(b + 1) * BT].rearrange("(t p) c -> p t c", p=P),
                             x_sb[:, b * TPB:(b + 1) * TPB]).then_inc(s_("out"), 16)
            sp.wait_ge(s_("out"), 16 * BLKS)

        @block.vector
        def _(v):
            ln_vector(v, 0)
            v.wait_ge(s_("cst_in"), 16)
            nc.vector.tensor_copy(cstb[:, 0:3 * P], cst[:, P:4 * P]).then_inc(s_("bf_cst"), 1)
            at = CST_AT["ida"]
            nc.vector.tensor_copy(cstb[:, 3 * P:], cst[:, at:at + 64 + SLOTS]).then_inc(s_("bf_cst"), 1)
            nc.vector.memset(kpz, 0.0).then_inc(s_("kpz"), 1)
            v.wait_ge(s_("kpz"), 1)
            v.wait_ge(s_("wqk_in"), 32)
            for g in range(2):
                nc.vector.tensor_scalar(kps[:, g, :], kpz, bqk0[:, 2 + g:3 + g], HD ** -0.5, ALU.add, ALU.mult)\
                    .then_inc(s_("kps_ready"), 1)
            with v.Fori(0, BLKS) as b:
                for g in range(2):
                    v.wait_ge(s_("k_mm"), b * 2 + g + 1)
                    src = ps[0:KC, 6 + g, :].rearrange("p (i y x) -> p i y x", i=2, y=SIDE)
                    blk = pt[g][0:KC, bass.ds(b * BT, BT)]
                    n0 = 2 * WA
                    outs = (blk[:, 0:n0].rearrange("p (i y x) -> p i y x", i=2, x=WS),
                            blk[:, n0:BT].rearrange("p (i n) -> p i n", i=2)[:, :, 0:NBD]
                            .rearrange("p i (y x) -> p i y x", x=SIDE - WS),
                            blk[:, n0:BT].rearrange("p (i n) -> p i n", i=2)[:, :, NBD:NB1]
                            .rearrange("p i (y x) -> p i y x", x=WS))
                    ins = (src[:, :, 0:WS, 0:WS], src[:, :, :, WS:SIDE], src[:, :, WS:SIDE, 0:WS])
                    for o, i in zip(outs, ins):
                        last = nc.vector.tensor_scalar(o, i, bqk0[:, 2 + g:3 + g], HD ** -0.5, ALU.add, ALU.mult)
                    last.then_inc(s_("k_free"), 1)
            v.wait_ge(s_("pk_hi"), 1)
            nc.vector.tensor_tensor(pk[R_DUP:R_DUP + HD], padf[R_DUP:R_DUP + HD],
                                    pk[R_DUP:R_DUP + HD].bitcast(F32), ALU.subtract).then_inc(s_("pk_ready"), 1)
            for k in range(2, 8):
                if k < 4:
                    v.wait_ge(s_("q_ready"), 2 + 2 * BLKS)
                    src, rows = qT[:, k - 2, :], KC
                else:
                    v.wait_ge(s_("rel_out"), 4 * (k - 3))
                    src, rows = rn[k % 2], HG * WS
                if k >= 3:
                    v.wait_ge(s_(f"stored{k - 3}"), 16)
                permute(pt[k % 3], src, rows).then_inc(s_("staged"), 1)
            attn0_vector(v)
            moe_vector(v, 0)
            attn1_vector(v)
            moe_vector(v, 1)

        @block.tensor
        def _(pe):
            pe.wait_ge(s_("cst_in"), 16)

            def queries_and_keys(b):
                pe.wait_ge(s_("tp_free"), b + 3)
                for m in range(4):
                    pe.wait_ge(s_("q_ready" if m < 2 else "k_free"), b * 2 + m % 2 + 1)
                    for k in range(2):
                        last = nc.tensor.matmul(ps[0:KC, 4 + m, :], wqk0[:, k, m, :],
                                                xnT_v[:, k, bass.ds(b * BT, BT)], start=k == 0, stop=k == 1)
                    last.then_inc(s_("q_mm" if m < 2 else "k_mm"), 1)

            ln_transpose(pe, 0, 0, 0)
            ln_transpose(pe, 0, 1, 1)
            pe.wait_ge(s_("wqk_in"), 32)
            queries_and_keys(0)
            ln_transpose(pe, 0, 2, 0)
            ln_transpose(pe, 0, 3, 1)
            with pe.Fori(1, BLKS) as b:
                queries_and_keys(b)
            pe.wait_ge(s_("rel_in"), 32)
            pe.wait_ge(s_("q_ready"), 2 + 2 * BLKS)
            for n in range(16):
                w, g, quarter = n // 8, n // 4 % 2, n % 4
                if n >= 4:
                    pe.wait_ge(s_("rel_out"), n - 3)
                img = qT[:, g, :].rearrange("p (i y x) -> p i y x", i=IMGS, y=SIDE)
                for u in range(4):
                    at = 4 * quarter + u
                    rhs = img[:, :, at, :] if w == 0 else img[:, :, :, at]
                    last = nc.tensor.matmul(ps[0:HG * WS, n % 4, u * P:(u + 1) * P], relt[w][:, at % WS, :], rhs,
                                            start=True, stop=True)
                last.then_inc(s_("rel_mm"), 1)
            attn0_tensor(pe)
            moe_tensor(pe, 0)
            attn1_tensor(pe)
            moe_tensor(pe, 1)

        @block.scalar
        def _(act):
            ln_scalar(act, 0)
            act.wait_ge(s_("cqk_in"), 32)
            with act.Fori(0, BLKS) as b:
                for g in range(2):
                    act.wait_ge(s_("q_mm"), b * 2 + g + 1)
                    nc.scalar.activation(qT[:, g, bass.ds(b * BT, BT)], ps[0:KC, 4 + g, :], ACT.Identity,
                                         bias=bqk0[:, g:g + 1]).then_inc(s_("q_ready"), 1)
                for dst, src in ((q0, cq), (k0, ck)):
                    nc.scalar.activation(dst[KC:R_MAX + 1, b],
                                         src[KC:R_MAX + 1].unsqueeze(1).broadcast_to([R_MAX + 1 - KC, HC, BT]),
                                         ACT.Copy).then_inc(s_("rows_set"), 1)
            act.wait_ge(s_("padf_in"), 64)
            act.wait_ge(s_("q_ready"), 2 + 2 * BLKS)
            nc.scalar.activation(pk[0:R_MAX + 1], padf[0:R_MAX + 1], ACT.Copy).then_inc(s_("pk_hi"), 1)
            for n in range(16):
                w, g, quarter = n // 8, n // 4 % 2, n % 4
                k = n // 4
                if k >= 2 and quarter == 0:
                    act.wait_ge(s_("staged"), k + 1)
                act.wait_ge(s_("rel_mm"), n + 1)
                src = ps[0:HG * WS, n % 4, :]
                if w == 0:
                    d = rn[k % 2][0:HG * WS].rearrange("p (i y x) -> p y i x", i=IMGS, y=SIDE)
                    s = src.rearrange("p (y i x) -> p y i x", y=4, i=IMGS)
                else:
                    d = rn[k % 2][0:HG * WS].rearrange("p (r x) -> p x r", x=SIDE)
                    s = src.rearrange("p (x r) -> p x r", x=4)
                nc.scalar.activation(d[:, 4 * quarter:4 * quarter + 4], s, ACT.Copy).then_inc(s_("rel_out"), 1)
            act.wait_ge(s_("staged"), 4)
            for u in range(2):
                nc.scalar.activation(fk[u][0:R_ROUND], ck[0:R_ROUND].unsqueeze(1).broadcast_to([R_ROUND, HC, BT]),
                                     ACT.Copy).then_inc(s_("fk_rows"), 1)
            attn0_scalar(act)
            moe_scalar(act, 0)
            attn1_scalar(act)
            moe_scalar(act, 1)

        @block.gpsimd
        def _(pool):
            for k, (name, n) in enumerate((("xn_free", 2), ("tp_free", 2), ("q_ready", 2),
                                           ("k_free", 2), ("pv_done", 1), ("qkv_staged", 2),
                                           ("misc_full", 1), ("misc_free", 1))):
                nc.gpsimd.memset(credit[0:1, k:k + 1], 0.0).then_inc(s_(name), n)
            attn0_pool(pool)
            moe_pool(pool, 0)
            attn1_pool(pool)
            moe_pool(pool, 1)


INPUTS = ["x", "cst", "wqk0", "bqk0", "cq", "ck", "cpad", "relh", "relw", "wv0", "bv0", "wqkv1", "wp0", "bp0", "wg0", "bg0",
          "wp1", "bp1", "wg1", "bg1", "w1_0", "w2_0", "b2_0", "w1_1", "w2_1", "b2_1"]


def layout(i):
    import numpy as np

    f = np.float32
    o = {"x": i["x"].reshape(T, C)}

    def halves(w):
        return np.ascontiguousarray(w.reshape(2, KC, -1).transpose(1, 0, 2))

    def rows(b):
        return np.ascontiguousarray(np.broadcast_to(b.reshape(1, -1), (P, b.size)))

    w, b = i["L0_conv_qkv_w"], i["L0_conv_qkv_b"]
    o["wqk0"] = halves(w[:2 * C].T).reshape(KC, 2, 4, KC)
    o["bqk0"] = np.ascontiguousarray(b[:2 * C].reshape(4, KC).T)
    o["wv0"], o["bv0"] = halves(w[2 * C:].T), rows(b[2 * C:])
    for name, r in (("relh", i["L0_conv_rel_pos_h"]), ("relw", i["L0_conv_rel_pos_w"])):
        t = np.zeros((HG, HD, WS, HG, WS), f)
        for h in range(HG):
            for q in range(WS):
                for k in range(WS):
                    t[h, :, q, h, k] = r[q - k + WS - 1]
        o[name] = t.reshape(KC, WS, HG * WS)
    o["wp0"], o["bp0"] = halves(i["L0_conv_proj_w"].T), rows(i["L0_conv_proj_b"])
    o["wp1"], o["bp1"] = halves(i["L1_conv_proj_w"].T), rows(i["L1_conv_proj_b"])
    wd = np.zeros((2, GCH, 2, 3 * GCH), f)
    for j in range(2):
        wd[j, :, j] = i["L1_conv_qkv_w"].T
    o["wqkv1"] = wd.reshape(KC, 3, KC)
    o["wg0"], o["bg0"] = halves(i["L0_ffn_Wg"]), rows(i["L0_ffn_bg"])
    o["wg1"], o["bg1"] = halves(i["L1_ffn_gate_w"].T), np.zeros((P, E), f)
    for l, n in enumerate((("L0_ffn_W1", "L0_ffn_b1", "L0_ffn_W2", "L0_ffn_b2"),
                           ("L1_ffn_w1", "L1_ffn_b1", "L1_ffn_w2", "L1_ffn_b2"))):
        w1 = np.zeros((E, KC + 1, 2, F), f)
        w1[:, :KC] = i[n[0]].reshape(E, 2, KC, F).transpose(0, 2, 1, 3)
        w1[:, KC, 0] = i[n[1]]
        o[f"w1_{l}"] = w1
        o[f"w2_{l}"] = np.ascontiguousarray(i[n[2]].reshape(E, FT, P, C).transpose(0, 2, 1, 3))
        o[f"b2_{l}"] = rows(i[n[3]])

    y, x = np.divmod(np.arange(PIX), SIDE)
    order = [(y < WS) & (x < WS), x >= WS, (y >= WS) & (x < WS)]
    own = np.concatenate([np.flatnonzero(m) for m in order])
    tok = np.concatenate([own[:WA], own[:WA], own[WA:], own[WA:]])
    img = np.concatenate([np.zeros(WA), np.ones(WA), np.zeros(NB1), np.ones(NB1)]).astype(int)
    win = (y // WS * 2 + x // WS)[tok]
    hot = np.zeros((2 * WS, BT), f)
    hot[(y % WS)[tok], np.arange(BT)] = 1
    hot[WS + (x % WS)[tok], np.arange(BT)] = 1

    def key_rows(k, hot):
        k[R_REL1:R_REL1 + HD], k[R_REL2:R_REL2 + 2 * WS - HD] = hot[:HD], hot[HD:]
        k[R_RELLO:R_RELLO + 2 * WS] = hot
        k[R_MAX] = 1

    cq, ck, cp = np.zeros((P, BT), f), np.zeros((P, BT), f), np.zeros((P, PADS), f)
    key_rows(ck, hot)
    py, px = np.divmod(np.arange(WA), WS)
    hot = np.zeros((2 * WS, PADS), f)
    hot[py, np.arange(WA)] = 1
    hot[WS + px, np.arange(WA)] = 1
    key_rows(cp, hot)
    edge = SIDE - WS
    for n in range(2):
        for m in range(1, 4):
            r = R_WIN + 3 * n + m - 1
            mine = (img == n) & (win == m)
            cq[r, mine] = NEG
            ck[r, 2 * WA:] = ~mine[2 * WA:]
            cp[r, :WA] = ((px < edge) | (m == 2)) & ((py < edge) | (m == 1))
            cp[r, WA:] = 1
    o["cq"], o["ck"], o["cpad"] = cq, ck, cp

    p, e, s = np.arange(P), np.arange(E), np.arange(SLOTS)
    token = np.arange(TILES)[None, :] * P + p[:, None]
    ids = np.stack([2 * token + k + 1 for k in range(2)], 1).reshape(P, -1)
    sel = np.zeros((P, KC), f)
    sel[KC + np.arange(KC) // HD, np.arange(KC)] = 1
    o["cst"] = np.concatenate([
        np.eye(P), p[:, None] < p[None, :], np.tile(p, (P, 1)), np.ones((P, P)), np.tile(E - e, (P, 1)),
        np.tile((e[None, :] < e[:, None]).reshape(-1), (P, 1)), ids // 64, ids % 64, np.tile(s, (P, 1)), sel], 1).astype(f)
    return {k: np.ascontiguousarray(o[k]) for k in INPUTS}


def kernel(**inputs):
    import numpy as np
    import concourse.bacc as bacc
    from concourse.bass_utils import run_bass_kernel_spmd

    arrays = layout({k: np.asarray(v) for k, v in inputs.items()})
    nc = bacc.Bacc("TRN2", target_bir_lowering=False, num_devices=1)
    aps = {k: nc.dram_tensor(f"in_{k}", v.shape, mybir.dt.from_np(v.dtype), kind="ExternalInput").ap()
           for k, v in arrays.items()}
    out = nc.dram_tensor("out_x", [T, C], F32, kind="ExternalOutput").ap()
    build(nc, aps, out)
    result = run_bass_kernel_spmd(nc, [{f"in_{k}": v for k, v in arrays.items()}], core_ids=[0])
    return result.results[0]["out_x"].reshape(IMGS, SIDE, SIDE, C)
```
